# Optimizing a Trainium2 kernel written in Bass

```python
import numpy as np
import jax
import jax.numpy as jnp

def _softmax(x, axis=-1):
    return jax.nn.softmax(x, axis=axis)

def _gelu(x):
    return jax.nn.gelu(x, approximate=True)

def _silu(x):
    return jax.nn.silu(x)

def _sigmoid(x):
    return jax.nn.sigmoid(x)

def _layernorm(x, axis=-1, eps=1e-05):
    m = jnp.mean(x, axis=axis, keepdims=True)
    v = jnp.var(x, axis=axis, keepdims=True)
    return (x - m) / jnp.sqrt(v + eps)

def _scatter_add(tgt, idx, src, axis=0):
    return tgt.at[idx].add(src)

def _segment_sum(src, seg, n):
    return jax.ops.segment_sum(src, seg, n)
kernel_name = 'mk_seq_postln_d1_jaxref_r8_17b564'

def setup_inputs(seed: int=0):
    np.random.seed(seed)
    _w = jnp.asarray

    def _L0_attn_setup():
        import jax, jax.numpy as jnp
        import numpy as np
        D_MODEL = 128
        N_HEADS = 8
        D_STATE = 64
        HEAD_DIM = 64
        EXPAND = 2
        D_INNER = N_HEADS * HEAD_DIM
        BATCH = 2
        SEQ = 512

        def _ssd_scan(X, delta, B_ssm, C_ssm, A_log):
            neg_A = -jnp.exp(A_log)

            def step(h, inp):
                X_t, d_t, B_t, C_t = inp
                dA = jnp.exp(d_t * neg_A)
                dB = d_t[..., None] * B_t[:, None, :]
                h = dA[..., None, None] * h + X_t[..., None] * dB[:, :, None, :]
                y_t = jnp.einsum('bhpn,bn->bhp', h, C_t)
                return (h, y_t)
            b, t, hh, p = X.shape
            n = B_ssm.shape[-1]
            h0 = jnp.zeros((b, hh, p, n), dtype=X.dtype)
            xs = (jnp.swapaxes(X, 0, 1), jnp.swapaxes(delta, 0, 1), jnp.swapaxes(B_ssm, 0, 1), jnp.swapaxes(C_ssm, 0, 1))
            h_last, ys = jax.lax.scan(step, h0, xs)
            return (jnp.swapaxes(ys, 0, 1), h_last)

        def _reference_tuple_inner(x, Wz, Win, Wzg, Wout, dt_bias, A_log, D_param):
            b, t, _ = x.shape
            z = x @ Wz
            ssm_in = x @ Win
            B_ssm = ssm_in[..., :D_STATE]
            C_ssm = ssm_in[..., D_STATE:2 * D_STATE]
            dt_raw = ssm_in[..., 2 * D_STATE:2 * D_STATE + N_HEADS]
            X = ssm_in[..., 2 * D_STATE + N_HEADS:].reshape(b, t, N_HEADS, HEAD_DIM)
            delta = jax.nn.softplus(dt_raw + dt_bias)
            y, h_last = _ssd_scan(X, delta, B_ssm, C_ssm, A_log)
            y = y + D_param[None, None, :, None] * X
            y_flat = y.reshape(b, t, D_INNER)
            z_gated = jax.nn.silu(z) @ Wzg
            output = y_flat * z_gated @ Wout
            return (output, h_last)
        key = jax.random.key(seed)
        ks = jax.random.split(key, 6)
        s = 0.02
        x = jax.random.normal(ks[0], (BATCH, SEQ, D_MODEL), dtype=jnp.float32)
        Wz = jax.random.normal(ks[1], (D_MODEL, D_MODEL * EXPAND), dtype=jnp.float32) * s
        Win = jax.random.normal(ks[2], (D_MODEL, 2 * D_STATE + N_HEADS + D_INNER), dtype=jnp.float32) * s
        Wzg = jax.random.normal(ks[3], (D_MODEL * EXPAND, D_INNER), dtype=jnp.float32) * s
        Wout = jax.random.normal(ks[4], (D_INNER, D_MODEL), dtype=jnp.float32) * s
        dt_bias = jnp.full((N_HEADS,), np.log(0.1), dtype=jnp.float32)
        A_log = jnp.log(jnp.arange(1, N_HEADS + 1, dtype=jnp.float32))
        D_param = jnp.ones((N_HEADS,), dtype=jnp.float32)
        return {'x': x, 'Wz': Wz, 'Win': Win, 'Wzg': Wzg, 'Wout': Wout, 'dt_bias': dt_bias, 'A_log': A_log, 'D_param': D_param}
    _L0_attn_in = _L0_attn_setup()

    def _L0_ffn_setup():
        import jax, jax.numpy as jnp
        import numpy as np
        K = 3
        TAU = 1.0
        EPS = 1e-08

        def _route_dense(z, k, tau):
            topi = jax.lax.top_k(z, k)[1]
            topv = jnp.take_along_axis(z, topi, axis=1)
            w = jax.nn.softmax(topv / (tau + EPS), axis=1)
            N, L = z.shape
            dw = jnp.zeros((N, L), z.dtype)
            dw = dw.at[jnp.arange(N)[:, None], topi].add(w)
            return dw

        def _apply_mixture(x, dw, W):
            y = jnp.zeros((x.shape[0], W.shape[1]), x.dtype)
            for e in range(W.shape[0]):
                y = y + x @ W[e].T * dw[:, e:e + 1]
            return y
        key = jax.random.key(seed)
        ks = jax.random.split(key, 8)
        B, T, D_in, H, D_out, L, d_addr = (4, 256, 128, 512, 128, 12, 64)

        def unitize(U):
            U = U - U.mean(axis=1, keepdims=True)
            return U / (jnp.linalg.norm(U, axis=1, keepdims=True) + EPS)
        x = jax.random.normal(ks[0], (B, T, D_in), jnp.float32)
        P_w = jax.random.normal(ks[1], (d_addr, D_in), jnp.float32) / np.sqrt(D_in)
        U1 = unitize(jax.random.normal(ks[2], (L, d_addr), jnp.float32))
        U2 = unitize(jax.random.normal(ks[3], (L, d_addr), jnp.float32))
        U3 = unitize(jax.random.normal(ks[4], (L, d_addr), jnp.float32))
        W1 = jax.random.normal(ks[5], (L, H, D_in), jnp.float32)
        W1 = W1 / jnp.linalg.norm(W1.reshape(L, -1), axis=1)[:, None, None]
        W2 = jax.random.normal(ks[6], (L, D_out, H), jnp.float32)
        W2 = W2 / jnp.linalg.norm(W2.reshape(L, -1), axis=1)[:, None, None]
        b2 = jax.random.normal(ks[7], (L, D_out), jnp.float32)
        b2 = b2 / jnp.linalg.norm(b2, axis=1, keepdims=True)
        return {'x': x, 'P_w': P_w, 'U1': U1, 'U2': U2, 'U3': U3, 'W1': W1, 'W2': W2, 'b2': b2}
    _L0_ffn_in = _L0_ffn_setup()
    _d = {'L0_attn_x': _L0_attn_in['x'], 'L0_attn_Wz': _L0_attn_in['Wz'], 'L0_attn_Win': _L0_attn_in['Win'], 'L0_attn_Wzg': _L0_attn_in['Wzg'], 'L0_attn_Wout': _L0_attn_in['Wout'], 'L0_attn_dt_bias': _L0_attn_in['dt_bias'], 'L0_attn_A_log': _L0_attn_in['A_log'], 'L0_attn_D_param': _L0_attn_in['D_param'], 'L0_ffn_P_w': _L0_ffn_in['P_w'], 'L0_ffn_U1': _L0_ffn_in['U1'], 'L0_ffn_U2': _L0_ffn_in['U2'], 'L0_ffn_U3': _L0_ffn_in['U3'], 'L0_ffn_W1': _L0_ffn_in['W1'], 'L0_ffn_W2': _L0_ffn_in['W2'], 'L0_ffn_b2': _L0_ffn_in['b2']}
    _x0 = _d['L0_attn_x']
    _d['L0_attn_x'] = jax.random.normal(jax.random.fold_in(jax.random.key(seed), 1), (16, 512, 128), dtype=_x0.dtype)
    del _x0
    return _d

def reference(L0_attn_x, L0_attn_Wz, L0_attn_Win, L0_attn_Wzg, L0_attn_Wout, L0_attn_dt_bias, L0_attn_A_log, L0_attn_D_param, L0_ffn_P_w, L0_ffn_U1, L0_ffn_U2, L0_ffn_U3, L0_ffn_W1, L0_ffn_W2, L0_ffn_b2):

    def _L0_attn_ref(x, Wz, Win, Wzg, Wout, dt_bias, A_log, D_param):
        import jax, jax.numpy as jnp
        import numpy as np
        D_MODEL = 128
        N_HEADS = 8
        D_STATE = 64
        HEAD_DIM = 64
        EXPAND = 2
        D_INNER = N_HEADS * HEAD_DIM
        BATCH = 2
        SEQ = 512

        def _ssd_scan(X, delta, B_ssm, C_ssm, A_log):
            neg_A = -jnp.exp(A_log)

            def step(h, inp):
                X_t, d_t, B_t, C_t = inp
                dA = jnp.exp(d_t * neg_A)
                dB = d_t[..., None] * B_t[:, None, :]
                h = dA[..., None, None] * h + X_t[..., None] * dB[:, :, None, :]
                y_t = jnp.einsum('bhpn,bn->bhp', h, C_t)
                return (h, y_t)
            b, t, hh, p = X.shape
            n = B_ssm.shape[-1]
            h0 = jnp.zeros((b, hh, p, n), dtype=X.dtype)
            xs = (jnp.swapaxes(X, 0, 1), jnp.swapaxes(delta, 0, 1), jnp.swapaxes(B_ssm, 0, 1), jnp.swapaxes(C_ssm, 0, 1))
            h_last, ys = jax.lax.scan(step, h0, xs)
            return (jnp.swapaxes(ys, 0, 1), h_last)

        def _reference_tuple_inner(x, Wz, Win, Wzg, Wout, dt_bias, A_log, D_param):
            b, t, _ = x.shape
            z = x @ Wz
            ssm_in = x @ Win
            B_ssm = ssm_in[..., :D_STATE]
            C_ssm = ssm_in[..., D_STATE:2 * D_STATE]
            dt_raw = ssm_in[..., 2 * D_STATE:2 * D_STATE + N_HEADS]
            X = ssm_in[..., 2 * D_STATE + N_HEADS:].reshape(b, t, N_HEADS, HEAD_DIM)
            delta = jax.nn.softplus(dt_raw + dt_bias)
            y, h_last = _ssd_scan(X, delta, B_ssm, C_ssm, A_log)
            y = y + D_param[None, None, :, None] * X
            y_flat = y.reshape(b, t, D_INNER)
            z_gated = jax.nn.silu(z) @ Wzg
            output = y_flat * z_gated @ Wout
            return (output, h_last)
        return _reference_tuple_inner(x, Wz, Win, Wzg, Wout, dt_bias, A_log, D_param)[0]

    def _L0_ffn_ref(x, P_w, U1, U2, U3, W1, W2, b2):
        import jax, jax.numpy as jnp
        import numpy as np
        K = 3
        TAU = 1.0
        EPS = 1e-08

        def _route_dense(z, k, tau):
            topi = jax.lax.top_k(z, k)[1]
            topv = jnp.take_along_axis(z, topi, axis=1)
            w = jax.nn.softmax(topv / (tau + EPS), axis=1)
            N, L = z.shape
            dw = jnp.zeros((N, L), z.dtype)
            dw = dw.at[jnp.arange(N)[:, None], topi].add(w)
            return dw

        def _apply_mixture(x, dw, W):
            y = jnp.zeros((x.shape[0], W.shape[1]), x.dtype)
            for e in range(W.shape[0]):
                y = y + x @ W[e].T * dw[:, e:e + 1]
            return y
        B, T, D = x.shape
        x_flat = x.reshape(B * T, D)
        x_addr = x_flat @ P_w.T
        dw1 = _route_dense(x_addr @ U1.T, K, TAU)
        dw2 = _route_dense(x_addr @ U2.T, K, TAU)
        dw3 = _route_dense(x_addr @ U3.T, K, TAU)
        h = _apply_mixture(x_flat, dw1, W1)
        h = jax.nn.gelu(h, approximate=False)
        y = _apply_mixture(h, dw2, W2)
        y = y + dw3 @ b2
        return y.reshape(B, T, -1)
    x = L0_attn_x
    x = _layernorm(x + _L0_attn_ref(x, L0_attn_Wz, L0_attn_Win, L0_attn_Wzg, L0_attn_Wout, L0_attn_dt_bias, L0_attn_A_log, L0_attn_D_param), axis=-1)
    x = _layernorm(x + _L0_ffn_ref(x, L0_ffn_P_w, L0_ffn_U1, L0_ffn_U2, L0_ffn_U3, L0_ffn_W1, L0_ffn_W2, L0_ffn_b2), axis=-1)
    return x

_drawn_inputs = setup_inputs


def setup_inputs(seed=0):
    import zlib

    import numpy as np

    out = dict(_drawn_inputs(seed))
    spreads = {'L0_attn_dt_bias': (-2.3025851249694824, 0.6), 'L0_attn_D_param': (1.0, 0.6)}
    factors = {'L0_attn_Wz': 8.0,
     'L0_attn_Win': 8.0,
     'L0_attn_Wzg': 8.0,
     'L0_attn_Wout': 8.0,
     'L0_attn_A_log': 8.0,
     'L0_ffn_U1': 8.0,
     'L0_ffn_U2': 8.0,
     'L0_ffn_W1': 8.0,
     'L0_ffn_W2': 8.0}
    for name, (base, spread) in spreads.items():
        noise = np.random.default_rng([zlib.crc32(name.encode()), seed]).standard_normal(out[name].shape)
        drawn = base * np.exp(spread * noise) if base else spread * noise
        out[name] = jnp.asarray(drawn.astype(out[name].dtype))
    for name, factor in factors.items():
        out[name] = (out[name] * factor).astype(out[name].dtype)
    return out
```

```python
from contextlib import ExitStack

import numpy as np

import concourse.bass as bass
from concourse import mybir

F32 = mybir.dt.float32
F32R = mybir.dt.float32r
I32 = mybir.dt.int32
U32 = mybir.dt.uint32
ALU = mybir.AluOpType
ACT = mybir.ActivationFunctionType
AX = mybir.AxisListType

P = 128
D = 128
NB, T = 16, 512
NC = T // P
H, HD, NS = 8, 64, 64
NQ = H // 2
DI = H * HD
DZ = 2 * D
NK = DZ // P
E, TOPK = 12, 3
HID = 512
NH = HID // P
NG = E * D // T
EG = E // NG
NR = 3
B2ROW = 32
DTROW = 64
LN_EPS = 1e-5

MIX_USES = (
    [("xT", "xT", 1), ("dtB", "dt_raw", 1), ("BC", "BC", 1)]
    + [(f"z{k}", "silu", k + 1) for k in range(NK)]
    + [(f"X{c}", "Xd", c + 1) for c in range(NC)]
    + [(f"zg{q}", "zg", q + 1) for q in range(NQ)]
    + [("G", "Gm", 1), ("cum", "cumexp", 1), ("ends", "ends", 1)]
    + [(f"st{c}", "state", c + 1) for c in range(NC - 1)]
    + [u for q in range(NQ) for u in (
        (f"decb{q}", "decb", q + 1), (f"seg{2 * q}", "segexp", 2 * q + 1), (f"seg{2 * q + 1}", "segexp", 2 * q + 2),
        (f"inter{q}", "inter", q + 1), (f"XT{q}", "skip", q + 1), (f"intra{q}", "y", q + 1))]
    + [("out", "v", 1)]
)
MIX_USE = {u[0]: n for n, u in enumerate(MIX_USES)}
NX = 3


class Batch:

    def __init__(self, reg, off):
        self.reg, self.off = reg, off

    def prev(self):
        return Batch(self.reg, self.off - 1)

    def index(self):
        if self.reg is None:
            return self.off
        return self.reg + self.off if self.off else self.reg


class Product:

    def __init__(self, sem, name, n, step=1):
        self.sem, self.name, self.n, self.step = sem, name, n, step
        self.done = 0


def layer_program(nc, x, Wz, Win, Wzg, Wout, dt_bias, A_log, D_param, P_w, U1T, U2T, U3T, W1T, W2T, b2, out):
    ctx = ExitStack()
    with ctx:
        def sb(name, shape, dt=F32):
            return ctx.enter_context(nc.sbuf_tensor(name, shape, dt))

        w1_hi, w1_lo = sb("w1_hi", [P, E, HID], F32R), sb("w1_lo", [P, E, HID], F32R)
        w2_hi, w2_lo = sb("w2_hi", [P, NH, E * D], F32R), sb("w2_lo", [P, NH, E * D], F32R)
        wbc_hi, wbc_lo = sb("wbc_hi", [P, 2 * NS], F32R), sb("wbc_lo", [P, 2 * NS], F32R)
        wz_hi, wz_lo = sb("wz_hi", [P, DZ], F32R), sb("wz_lo", [P, DZ], F32R)
        wx_hi, wx_lo = sb("wx_hi", [P, DI], F32R), sb("wx_lo", [P, DI], F32R)
        wzg_hi, wzg_lo = sb("wzg_hi", [P, NK, DI], F32R), sb("wzg_lo", [P, NK, DI], F32R)
        wbdt = sb("wbdt", [P, P])
        wout = sb("wout", [P, NQ, D])
        router = sb("router", [P, P])
        b2_sb = sb("b2_sb", [NS, D])
        ident, upper = sb("ident", [P, P]), sb("upper", [P, P])
        strict = sb("strict", [P, P])
        strict_r = sb("strict_r", [P, P], F32R)
        pick_f, pick = sb("pick_f", [P, E]), sb("pick", [P, E], F32R)
        pairs = sb("pairs", [P, DI], F32R)
        iota_i, iota_e = sb("iota_i", [P, E], I32), sb("iota_e", [P, E])
        bias_b, neg_a, d_col = sb("bias_b", [P, H]), sb("neg_a", [P, H]), sb("d_col", [P, NQ])
        x_in = sb("x_in", [P, NC, D])
        resid = sb("resid", [P, NC, D])
        xT = sb("xT", [P, T])
        xT_hi, xT_lo = sb("xT_hi", [P, T], F32R), sb("xT_lo", [P, T], F32R)
        BT, CT = sb("BT", [NS, T]), sb("CT", [NS, T])
        B_tok = sb("B_tok", [P, NC, NS])
        Xd = sb("Xd", [P, NC, DI])
        Ua_hi, Ua_lo = sb("Ua_hi", [P, T], F32R), sb("Ua_lo", [P, T], F32R)
        Gm = sb("Gm", [P, NC, P])
        Wt = sb("Wt", [P, 2, 2 * T])
        S = sb("S", [NS, NC - 1, DI])
        pw, ut = S[:, 0, 0:D], S[:, 0, D:2 * D]
        decb = sb("decb", [P, T])
        yt = sb("yt", [P, T])
        zg = sb("zg", [P, NQ, T])
        dt_s = sb("dt_s", [P, 6, NC * H])
        delta, a, a_lo = sb("delta", [P, NC, H]), sb("a", [P, NC, H]), sb("a_lo", [P, NC, H])
        a_hi = sb("a_hi", [P, NC, H], F32R)
        ends = sb("ends", [P, (NC - 1) * H])
        total = sb("total", [NS, NC * H])
        silu = Wt[:, 0, :].rearrange("p (k t) -> p k t", k=NK)
        pairs_f = Wt[:, 1, 0:DI]
        Xde = Wt[:, :, :].rearrange("p a b -> p (a b)")[:, 0:(NC - 1) * DI].rearrange("p (c n) -> p c n", c=NC - 1)
        rows = sb("rows", [P, T])
        rows_hi, rows_lo = sb("rows_hi", [P, T], F32R), sb("rows_lo", [P, T], F32R)
        fbuf = sb("fbuf", [P, 4, T])
        x1 = fbuf[:, 0, :].rearrange("p (c d) -> p c d", c=NC)
        x1T = fbuf[:, 1, :]
        o_sb = fbuf[:, 1, :].rearrange("p (c d) -> p c d", c=NC)
        wide = [fbuf[:, 2, :], fbuf[:, 3, :]]
        sp_hi, sp_lo = sb("sp_hi", [P, NH, T], F32R), sb("sp_lo", [P, NH, T], F32R)
        lg = fbuf[:, 3, 0:NC * NR * E].rearrange("p (g e) -> p g e", e=E)
        mx = fbuf[:, 3, NC * NR * E:NC * NR * (E + 8)].rearrange("p (g e) -> p g e", e=8)
        ix = sb("ix", [P, NC * NR, 8], U32)
        hot = fbuf[:, 2, 0:TOPK * NC * NR * E].rearrange("p (k g e) -> p k g e", k=TOPK, g=NC * NR)
        ssum, srec = sb("ssum", [P, NC * NR]), sb("srec", [P, NC * NR])
        dw2 = sb("dw2", [P, NC, E])
        dwpad = sb("dwpad", [P, NC, DTROW])
        st6, mv, nrm = sb("st6", [P, NC, 6]), sb("mv", [P, NC, 2]), sb("nrm", [P, 6, NC])

        xb = [ctx.enter_context(nc.psum_tensor(f"mix_bank{n}", [P, T], F32)) for n in range(NX)]
        hb = [ctx.enter_context(nc.psum_tensor(f"exp_bank{n}", [P, T], F32)) for n in range(NH)]
        rb = ctx.enter_context(nc.psum_tensor("row_bank", [P, T], F32))

        prods = {}

        def product(name, n, step=1):
            prods[name] = Product(ctx.enter_context(nc.semaphore(name)), name, n, step)

        for name, n in dict(
            ps_xT=1, xT=1, xT_lo=1, ps_dtB=1, B_tok=1, dt_raw=1, dt_v=13, dt_s=2, a_split=2, ps_BC=1, BC=1,
            copied=1, ps_z=NK, tanh=NK, silu=NK, silu_hi=NK, silu_lo=NK, ps_X=NC, Xd=NC, ps_zg=NQ, zg=NQ,
            ps_G=1, Gm=1, ps_cum=1, cumexp=1, cum_hi=1, cum_lo=1, ps_ends=1, ends=1, Xde=NC - 1,
            ps_st=NC - 1, state=NC - 1, st_tmp=NC - 2, ps_decb=NQ, decb=NQ, Ua=2 * NQ, ps_seg=2 * NQ, segexp=2 * NQ,
            W=2 * NQ, ps_inter=NQ, inter=NQ, ps_XT=NQ, skip=NQ, ps_intra=NQ, y=NQ, gated=NQ, ps_out=1, v=1,
            ln1_v=7, ln1_s=2, x1=1, ps_x1T=1, x1T=1, ps_lg=1, lg=1, rt_v=8, rt_s=1, dw=1, ps_dwT=1, dwT=1, dw_hi=1,
            dw_lo=1, ps_row=E, xw=E, xw_hi=E, xw_lo=E, ps_h=E, gelu=NH, gelu_hi=NH, gelu_lo=NH, ps_b2=1, acc=1,
            ps_y=NC * NG, comb=NC * E, ln2_v=7, ln2_s=2, o=1,
        ).items():
            product(name, n)
        product("x_in", 1, 16)
        product("stored", 1, 16)
        sems = {n: ctx.enter_context(nc.semaphore("set_" + n)) for n in
                ("mix_w", "small", "ring0", "ring1", "ring2", "ring3", "w_hi", "w_lo", "masks", "cast", "chain", "alog", "ps_r", "router", "pad")}

        waited = {}

        def wait(eng, name, b, k=None):
            p = prods[name]
            v = b.off * p.n * p.step + (p.n if k is None else k) * p.step
            seen = waited.setdefault(id(eng), {})
            if (b.reg is None and v <= 0) or seen.get(name, -10**9) >= v:
                return
            seen[name] = v
            eng.wait_ge(p.sem, v if b.reg is None else b.reg * (p.n * p.step) + v)

        def alone(eng):
            eng.nop(nofuse=True)

        def sig(name, ins):
            p = prods[name]
            p.done += 1
            ins.then_inc(p.sem, p.step)

        def link(eng, name, b, ins, count):
            count[0] += 1
            sig(name, ins)
            wait(eng, name, b, count[0])

        def mm3(ps, pairs, start=True, stop=True):
            last = None
            n = len(pairs)
            for j, (s_hi, s_lo, m_hi, m_lo) in enumerate(pairs):
                nc.tensor.matmul(ps, s_hi, m_hi, start=start and j == 0, stop=False)
                nc.tensor.matmul(ps, s_hi, m_lo, start=False, stop=False)
                last = nc.tensor.matmul(ps, s_lo, m_hi, start=False, stop=stop and j == n - 1)
            return last

        def mix_bank(b, use):
            n = MIX_USE[use]
            if n >= NX:
                before, owner = n - NX, b
            else:
                before, owner = max(m for m in range(len(MIX_USES)) if m % NX == n), b.prev()
            _, reader, k = MIX_USES[before]
            wait(nc.tensor, reader, owner, k)
            return xb[n % NX]

        def bank_of(use):
            return xb[MIX_USE[use] % NX]

        tok = lambda c: slice(c * P, (c + 1) * P)
        PE, DVE, AC, PO, SP = nc.tensor, nc.vector, nc.scalar, nc.gpsimd, nc.sync

        NW = 2 * E
        RING = 4
        mix_stage = Xd[:, :, :].rearrange("p c n -> p (c n)")
        st_win, st_wz = mix_stage[:, 0:648], mix_stage[:, 648:904]
        st_wzg = mix_stage[:, 904:904 + NK * DI].rearrange("p (k n) -> p k n", k=NK)

        def w_tile(k):
            if k < E:
                return W1T[:, k, :], w1_hi[:, k, :], w1_lo[:, k, :]
            kc, g = divmod(k - E, NG)
            cols = slice(g * T, (g + 1) * T)
            return W2T[kc * P:(kc + 1) * P, cols], w2_hi[:, kc, cols], w2_lo[:, kc, cols]

        def setup(eng):
            if eng is SP:
                SP.dma_start(x_in[:, :, :], x[0].rearrange("(c p) d -> p c d", p=P)).then_inc(prods["x_in"].sem, 16)
                SP.dma_start(st_win, Win[:, :]).then_inc(sems["mix_w"], 16)
                SP.dma_start(st_wz, Wz[:, :]).then_inc(sems["mix_w"], 16)
                SP.dma_start(st_wzg, Wzg.rearrange("(k p) n -> p k n", p=P)).then_inc(sems["mix_w"], 16)
                SP.wait_ge(sems["pad"], 2)
                SP.dma_start(wbdt[:, 0:NS], Win[:, 0:NS]).then_inc(sems["small"], 16)
                SP.dma_start(wbdt[:, NS:NS + H], Win[:, 2 * NS:2 * NS + H]).then_inc(sems["small"], 16)
                SP.dma_start(bias_b[:, :], dt_bias.partition_broadcast(P)).then_inc(sems["small"], 16)
                SP.dma_start(neg_a[:, :], A_log.partition_broadcast(P)).then_inc(sems["small"], 16)
                for j in range(2):
                    SP.dma_start(d_col[j * HD:(j + 1) * HD, :],
                                 D_param.rearrange("(q j) -> j q", j=2)[j, :].partition_broadcast(HD),
                                 allow_slow_non_contiguous=True).then_inc(sems["small"], 16)
                SP.dma_start(wout[:, :, :], Wout.rearrange("(q p) n -> p q n", p=P)).then_inc(sems["small"], 16)
                SP.dma_start(pw, P_w[:, :]).then_inc(sems["small"], 16)
                for r, u in enumerate((U1T, U2T, U3T)):
                    SP.dma_start(ut[:, r * E:(r + 1) * E], u[:, :]).then_inc(sems["small"], 16)
                SP.dma_start(b2_sb[B2ROW:B2ROW + E, :], b2[:, :]).then_inc(sems["small"], 16)
                for k in range(NW):
                    if k >= RING:
                        SP.wait_ge(sems["w_hi"], k - RING + 1)
                        SP.wait_ge(sems["w_lo"], k - RING + 1)
                        SP.wait_ge(sems[f"ring{k % RING}"], 16 * (k // RING))
                    SP.dma_start(fbuf[:, k % RING, :], w_tile(k)[0]).then_inc(sems[f"ring{k % RING}"], 16)
            if eng is PO:
                PO.memset(wbdt[:, :], 0.0).then_inc(sems["pad"], 1)
                PO.memset(ut, 0.0).then_inc(sems["pad"], 1)
                for m, v in ((ident, 0.0), (upper, 1.0), (strict, 1.0)):
                    PO.memset(m[:, :], v).then_inc(sems["masks"], 1)
                PO.memset(pick_f[:, :], 0.0).then_inc(sems["masks"], 1)
                PO.memset(pairs_f, 0.0).then_inc(sems["masks"], 1)
                PO.memset(dwpad[:, :, :], 0.0).then_inc(sems["masks"], 1)
                PO.memset(decb[:, 0:P], 0.0).then_inc(sems["masks"], 1)
                PO.iota(iota_i[:, :], pattern=[[1, E]], base=0, channel_multiplier=0).then_inc(sems["masks"], 1)
                PO.wait_ge(sems["masks"], 8)
                PO.affine_select(out=ident[:, :], in_=ident[:, :], compare_op=ALU.not_equal, fill=1.0, base=0,
                                 pattern=[[-1, P]], channel_multiplier=1).then_inc(sems["masks"], 1)
                PO.affine_select(out=upper[:, :], in_=upper[:, :], compare_op=ALU.is_ge, fill=0.0, base=0,
                                 pattern=[[1, P]], channel_multiplier=-1).then_inc(sems["masks"], 1)
                PO.affine_select(out=strict[:, :], in_=strict[:, :], compare_op=ALU.is_gt, fill=0.0, base=0,
                                 pattern=[[-1, P]], channel_multiplier=1).then_inc(sems["masks"], 1)
                PO.affine_select(out=pick_f[:, :], in_=pick_f[:, :], compare_op=ALU.not_equal, fill=1.0, base=0,
                                 pattern=[[-1, E]], channel_multiplier=1).then_inc(sems["masks"], 1)
                PO.affine_select(out=pairs_f, in_=pairs_f, compare_op=ALU.not_equal, fill=1.0, base=-DTROW,
                                 pattern=[[-1, H], [0, HD]], channel_multiplier=1).then_inc(sems["masks"], 1)
            if eng is DVE:
                DVE.wait_ge(sems["mix_w"], 48)
                DVE.tensor_scalar(st_wzg, st_wzg, 0.5, None, ALU.mult).then_inc(sems["chain"], 1)
                DVE.wait_ge(sems["chain"], 1)
                parts = ((st_win[:, 0:2 * NS], wbc_hi[:, :], wbc_lo[:, :]), (st_wz, wz_hi[:, :], wz_lo[:, :]),
                         (st_win[:, 2 * NS + H:], wx_hi[:, :], wx_lo[:, :]),
                         (st_wzg, wzg_hi[:, :, :], wzg_lo[:, :, :]))
                for src, hi, _ in parts:
                    last = DVE.tensor_copy(hi, src)
                last.then_inc(sems["chain"], 1)
                DVE.wait_ge(sems["chain"], 2)
                for src, hi, lo in parts:
                    DVE.tensor_tensor(lo, src, hi.bitcast(F32), ALU.subtract).then_inc(sems["cast"], 1)
                DVE.wait_ge(sems["masks"], 13)
                DVE.tensor_copy(strict_r[:, :], strict[:, :]).then_inc(sems["cast"], 1)
                DVE.tensor_copy(pick[:, :], pick_f[:, :]).then_inc(sems["cast"], 1)
                DVE.tensor_copy(pairs[:, :], pairs_f).then_inc(sems["cast"], 1)
                DVE.tensor_copy(iota_e[:, :], iota_i[:, :]).then_inc(sems["cast"], 1)
                DVE.wait_ge(sems["cast"], 8)
                DVE.wait_ge(sems["alog"], 1)
                DVE.tensor_scalar(neg_a[:, :], neg_a[:, :], -1.0, None, ALU.mult).then_inc(sems["chain"], 1)
                DVE.wait_ge(sems["chain"], 3)
                DVE.wait_ge(sems["ps_r"], 1)
                DVE.tensor_copy(router[:, :], rb[:, 0:P]).then_inc(sems["router"], 1)
            if eng is AC:
                AC.wait_ge(sems["small"], 16 * 12)
                AC.activation(neg_a[:, :], neg_a[:, :], ACT.Exp).then_inc(sems["alog"], 1)
            if eng is PE:
                PE.wait_ge(sems["small"], 16 * 12)
                PE.wait_ge(sems["masks"], 13)
                PE.wait_ge(sems["pad"], 2)
                PE.matmul(rb[:, 0:P], pw, ut, start=True, stop=True).then_inc(sems["ps_r"], 1)
                PE.wait_ge(sems["cast"], 8)

        def split_expert_weights(eng, ks):
            for k in ks:
                _, hi, lo = w_tile(k)
                if eng is AC:
                    AC.wait_ge(sems[f"ring{k % RING}"], 16 * (k // RING + 1))
                    AC.copy(hi, fbuf[:, k % RING, :]).then_inc(sems["w_hi"], 1)
                if eng is PO:
                    PO.wait_ge(sems["w_hi"], k + 1)
                    PO.tensor_tensor(lo, fbuf[:, k % RING, :], hi.bitcast(F32), ALU.subtract).then_inc(sems["w_lo"], 1)

        def expert_weights_ready(eng):
            if eng in (PE, DVE, AC):
                eng.wait_ge(sems["w_lo"], NW)
                eng.wait_ge(sems["w_hi"], NW)
            if eng is PE:
                eng.wait_ge(sems["router"], 1)

        def mix_x(eng, b):
            if eng is PE:
                wait(PE, "x_in", b)
                ps = mix_bank(b, "xT")
                for c in range(NC):
                    last = PE.transpose(ps[:, tok(c)], x_in[:, c, :], ident[:, :])
                sig("ps_xT", last)
            if eng is AC:
                wait(AC, "ps_xT", b)
                wait(AC, "ps_XT", b.prev())
                AC.copy(xT_hi[:, :], bank_of("xT")[:, :])
                sig("xT", AC.copy(xT[:, :], bank_of("xT")[:, :]))
            if eng is DVE:
                wait(DVE, "xT", b)
                wait(DVE, "ps_XT", b.prev())
                sig("xT_lo", DVE.tensor_tensor(xT_lo[:, :], xT[:, :], xT_hi[:, :].bitcast(F32), ALU.subtract))

        def mix_dt(eng, b):
            if eng is PE:
                wait(PE, "xT", b)
                ps = mix_bank(b, "dtB")
                for c in range(NC):
                    last = PE.matmul(ps[:, tok(c)], xT[:, tok(c)], wbdt[:, :], start=True, stop=True)
                sig("ps_dtB", last)
            ps = bank_of("dtB")[:, :].rearrange("p (c n) -> p c n", c=NC)
            e, u, den, one, m, q = (dt_s[:, n, :] for n in range(6))
            if eng is AC:
                wait(AC, "ps_dtB", b)
                wait(AC, "ps_st", b.prev())
                sig("B_tok", AC.copy(B_tok[:, :, :], ps[:, :, 0:NS]))
                wait(AC, "dt_v", b, 1)
                sig("dt_s", AC.activation(e, e, ACT.Exp))
                wait(AC, "dt_v", b, 2)
                sig("dt_s", AC.activation(m, u, ACT.Ln))
            if eng is DVE:
                wait(DVE, "ps_dtB", b)
                wait(DVE, "B_tok", b)
                n = [0]
                flat = delta[:, :, :].rearrange("p c h -> p (c h)")
                wait(DVE, "Xd", b.prev())
                sig("dt_raw", DVE.tensor_tensor(delta[:, :, :], ps[:, :, NS:NS + H],
                                                bias_b[:, :].unsqueeze(1).to_broadcast([P, NC, H]), ALU.add))
                wait(DVE, "dt_raw", b)
                link(DVE, "dt_v", b, DVE.scalar_tensor_tensor(e, flat, -1.0, flat, ALU.mult, ALU.min), n)
                wait(DVE, "dt_s", b, 1)
                link(DVE, "dt_v", b, DVE.tensor_scalar(u, e, 1.0, None, ALU.add), n)
                link(DVE, "dt_v", b, DVE.tensor_scalar(den, u, -1.0, None, ALU.add), n)
                link(DVE, "dt_v", b, DVE.tensor_scalar(one, den, 0.0, None, ALU.is_equal), n)
                link(DVE, "dt_v", b, DVE.tensor_tensor(den, den, one, ALU.add), n)
                link(DVE, "dt_v", b, DVE.reciprocal(q, den), n)
                link(DVE, "dt_v", b, DVE.tensor_tensor(q, q, e, ALU.mult), n)
                wait(DVE, "dt_s", b, 2)
                link(DVE, "dt_v", b, DVE.tensor_tensor(q, q, m, ALU.mult), n)
                link(DVE, "dt_v", b, DVE.tensor_tensor(one, one, e, ALU.mult), n)
                link(DVE, "dt_v", b, DVE.tensor_tensor(q, q, one, ALU.add), n)
                link(DVE, "dt_v", b, DVE.scalar_tensor_tensor(flat, flat, 0.0, q, ALU.max, ALU.add), n)
                wait(DVE, "ps_ends", b.prev())
                wait(DVE, "Ua", b.prev())
                link(DVE, "dt_v", b, DVE.tensor_tensor(
                    a[:, :, :], delta[:, :, :], neg_a[:, :].unsqueeze(1).to_broadcast([P, NC, H]), ALU.mult), n)
                link(DVE, "dt_v", b, DVE.tensor_copy(a_hi[:, :, :], a[:, :, :]), n)
                n2 = [0]
                link(DVE, "a_split", b, DVE.tensor_tensor(
                    a_lo[:, :, :], a[:, :, :], a_hi[:, :, :].bitcast(F32), ALU.subtract), n2)
                link(DVE, "a_split", b, DVE.tensor_copy(dt_s[:, 0, 0:1], dt_s[:, 0, 0:1]), n2)

        def mix_bc(eng, b):
            if eng is PE:
                wait(PE, "xT_lo", b)
                ps = mix_bank(b, "BC")
                sig("ps_BC", mm3(ps[:, :], [(wbc_hi[:, :], wbc_lo[:, :], xT_hi[:, :], xT_lo[:, :])]))
            if eng is AC:
                wait(AC, "ps_BC", b)
                wait(AC, "ps_G", b.prev())
                wait(AC, "ps_inter", b.prev())
                AC.copy(BT[:, :], bank_of("BC")[0:NS, :])
                sig("BC", AC.copy(CT[:, :], bank_of("BC")[NS:2 * NS, :]))

        def mix_keep_x(eng, b):
            if eng is PO:
                wait(PO, "x_in", b)
                wait(PO, "x1", b.prev())
                alone(PO)
                sig("copied", PO.tensor_copy(resid[:, :, :], x_in[:, :, :]))

        def mix_load_next(eng, b):
            if eng is SP:
                nxt = Batch(b.reg, b.off + 1)
                wait(SP, "ps_xT", b)
                wait(SP, "copied", b)
                sig("x_in", SP.dma_start(x_in[:, :, :], x_rows(nxt)))

        def x_rows(b):
            return x[b.index()].rearrange("(c p) d -> p c d", p=P) if b.reg is None else \
                x[bass.ds(b.index(), 1), :, :].rearrange("o (c p) d -> p (o c) d", p=P)

        def out_rows(b):
            return out[b.index()].rearrange("(c p) d -> p c d", p=P) if b.reg is None else \
                out[bass.ds(b.index(), 1), :, :].rearrange("o (c p) d -> p (o c) d", p=P)

        def mix_z(eng, b):
            for k in range(NK):
                if eng is PE:
                    wait(PE, "xT_lo", b)
                    ps = mix_bank(b, f"z{k}")
                    w = slice(k * P, (k + 1) * P)
                    sig("ps_z", mm3(ps[:, :], [(wz_hi[:, w], wz_lo[:, w], xT_hi[:, :], xT_lo[:, :])]))
                if eng is AC:
                    wait(AC, "ps_z", b, k + 1)
                    wait(AC, "ps_intra", b.prev())
                    sig("tanh", AC.activation(silu[:, k, :], bank_of(f"z{k}")[:, :], ACT.Tanh, scale=0.5))
                if eng is DVE:
                    wait(DVE, "tanh", b, k + 1)
                    sig("silu", DVE.scalar_tensor_tensor(silu[:, k, :], silu[:, k, :], 1.0, bank_of(f"z{k}")[:, :],
                                                         ALU.add, ALU.mult))
                    wait(DVE, "silu", b, k + 1)
                    wait(DVE, "ps_y", b.prev().prev())
                    sig("silu_hi", DVE.tensor_copy(sp_hi[:, k, :], silu[:, k, :]))
                if eng is PO:
                    wait(PO, "silu_hi", b, k + 1)
                    sig("silu_lo", PO.tensor_tensor(sp_lo[:, k, :], silu[:, k, :], sp_hi[:, k, :].bitcast(F32),
                                                    ALU.subtract))

        def mix_X(eng, b):
            for c in range(NC):
                if eng is PE:
                    ps = mix_bank(b, f"X{c}")
                    sig("ps_X", mm3(ps[:, :], [(xT_hi[:, tok(c)], xT_lo[:, tok(c)], wx_hi[:, :], wx_lo[:, :])]))
                if eng is DVE:
                    wait(DVE, "ps_X", b, c + 1)
                    wait(DVE, "ps_intra", b.prev())
                    wait(DVE, "a_split", b)
                    sig("Xd", DVE.tensor_tensor(
                        Xd[:, c, :].rearrange("p (h n) -> p h n", h=H),
                        bank_of(f"X{c}")[:, :].rearrange("p (h n) -> p h n", h=H),
                        delta[:, c, :].unsqueeze(2).to_broadcast([P, H, HD]), ALU.mult))

        def mix_zg(eng, b):
            for q in range(NQ):
                if eng is PE:
                    wait(PE, "silu_lo", b)
                    ps = mix_bank(b, f"zg{q}")
                    w = slice(q * P, (q + 1) * P)
                    sig("ps_zg", mm3(ps[:, :], [(wzg_hi[:, k, w], wzg_lo[:, k, w], sp_hi[:, k, :], sp_lo[:, k, :])
                                                for k in range(NK)]))
                if eng is AC:
                    wait(AC, "ps_zg", b, q + 1)
                    wait(AC, "ps_out", b.prev())
                    sig("zg", AC.copy(zg[:, q, :], bank_of(f"zg{q}")[:, :]))

        def mix_scores(eng, b):
            if eng is PE:
                wait(PE, "BC", b)
                ps = mix_bank(b, "G")
                for c in range(NC):
                    last = PE.matmul(ps[:, tok(c)], BT[:, tok(c)], CT[:, tok(c)], start=True, stop=True)
                sig("ps_G", last)
                wait(PE, "a_split", b)
                ps = mix_bank(b, "cum")
                for c in range(1, NC):
                    last = PE.matmul(ps[DTROW:DTROW + H, tok(c - 1)], a[:, c, :], upper[:, :], start=True, stop=True)
                sig("ps_cum", last)
                ps = mix_bank(b, "ends")
                PE.matmul(ps[:, 0:(NC - 1) * H], strict[:, :], a[:, 0:NC - 1, :].rearrange("p c h -> p (c h)"),
                          start=True, stop=True)
                sig("ps_ends", PE.matmul(ps[0:NS, 64:64 + NC * H], upper[:, P - 1:P].to_broadcast([P, NS]), a[:, :, :].rearrange("p c h -> p (c h)"),
                                         start=True, stop=True))
            R = slice(DTROW, DTROW + H)
            cols = (NC - 1) * P
            if eng is DVE:
                wait(DVE, "ps_G", b)
                wait(DVE, "W", b.prev())
                sig("Gm", DVE.tensor_tensor(Gm[:, :, :], bank_of("G")[:, :].rearrange("p (c t) -> p c t", c=NC),
                                            upper[:, :].unsqueeze(1).to_broadcast([P, NC, P]), ALU.mult))
                wait(DVE, "cumexp", b)
                wait(DVE, "ps_decb", b.prev())
                sig("cum_hi", DVE.tensor_copy(rows_hi[R, 0:cols], rows[R, 0:cols]))
                wait(DVE, "cum_hi", b)
                sig("cum_lo", DVE.tensor_tensor(rows_lo[R, 0:cols], rows[R, 0:cols], rows_hi[R, 0:cols].bitcast(F32),
                                                ALU.subtract))
            if eng is AC:
                wait(AC, "ps_cum", b)
                wait(AC, "cum_lo", b.prev())
                sig("cumexp", AC.activation(rows[R, 0:cols], bank_of("cum")[R, 0:cols], ACT.Exp))
                wait(AC, "ps_ends", b)
                wait(AC, "Xde", b.prev())
                wait(AC, "state", b.prev())
                AC.activation(ends[:, :], bank_of("ends")[:, 0:(NC - 1) * H], ACT.Exp)
                sig("ends", AC.activation(total[:, :], bank_of("ends")[0:NS, 64:64 + NC * H], ACT.Exp))
            if eng is PO:
                for c in range(NC - 1):
                    wait(PO, "ends", b)
                    wait(PO, "Xd", b, c + 1)
                    wait(PO, "silu_lo", b)
                    sig("Xde", PO.tensor_tensor(
                        Xde[:, c, :].rearrange("p (h n) -> p h n", h=H), Xd[:, c, :].rearrange("p (h n) -> p h n", h=H),
                        ends[:, c * H:(c + 1) * H].unsqueeze(2).to_broadcast([P, H, HD]), ALU.mult))

        def mix_states(eng, b):
            for c in range(NC - 1):
                if eng is PE:
                    wait(PE, "Xde", b, c + 1)
                    ps = mix_bank(b, f"st{c}")
                    sig("ps_st", PE.matmul(ps[0:NS, :], B_tok[:, c, :], Xde[:, c, :], start=True, stop=True))
                if eng is DVE:
                    wait(DVE, "ps_st", b, c + 1)
                    wait(DVE, "ps_inter", b.prev())
                    if c == 0:
                        sig("state", DVE.tensor_copy(S[:, 0, :], bank_of("st0")[0:NS, :]))
                    else:
                        wait(DVE, "state", b, c)
                        sig("st_tmp", DVE.tensor_tensor(
                            S[:, c, :].rearrange("p (h n) -> p h n", h=H),
                            S[:, c - 1, :].rearrange("p (h n) -> p h n", h=H),
                            total[:, c * H:(c + 1) * H].unsqueeze(2).to_broadcast([NS, H, HD]), ALU.mult))
                        wait(DVE, "st_tmp", b, c)
                        sig("state", DVE.tensor_tensor(S[:, c, :], S[:, c, :], bank_of(f"st{c}")[0:NS, :], ALU.add))

        def mix_pair(eng, b, q):
            HF = NC // 2
            for f in range(2):
                u = 2 * q + f
                cs = slice(f * HF, (f + 1) * HF)
                if eng is PO:
                    wait(PO, "a_split", b)
                    wait(PO, "ps_seg", b if u else b.prev(), u if u else None)
                    shape = [P, HF, 2, P]
                    up = upper[:, :].unsqueeze(1).unsqueeze(1).to_broadcast(shape)
                    for dst, src in ((Ua_hi, a_hi[:, cs, 2 * q:2 * q + 2].bitcast(F32)), (Ua_lo, a_lo[:, cs, 2 * q:2 * q + 2])):
                        last = PO.tensor_tensor(dst[:, :].rearrange("p (c j t) -> p c j t", c=HF, j=2), up,
                                                src.unsqueeze(3).to_broadcast(shape), ALU.mult)
                    sig("Ua", last)
            if eng is PE:
                wait(PE, "cum_lo", b)
                ps = mix_bank(b, f"decb{q}")
                cols = (NC - 1) * P
                R = slice(DTROW, DTROW + H)
                sel = pairs[R, q * P:(q + 1) * P]
                PE.matmul(ps[:, 0:cols], sel, rows_hi[R, 0:cols], start=True, stop=False)
                sig("ps_decb", PE.matmul(ps[:, 0:cols], sel, rows_lo[R, 0:cols], start=False, stop=True))
                for f in range(2):
                    u = 2 * q + f
                    wait(PE, "Ua", b, u + 1)
                    ps = mix_bank(b, f"seg{u}")
                    PE.matmul(ps[:, :], strict_r[:, :], Ua_hi[:, :], start=True, stop=False)
                    sig("ps_seg", PE.matmul(ps[:, :], strict_r[:, :], Ua_lo[:, :], start=False, stop=True))
                wait(PE, "state", b)
                ps = mix_bank(b, f"inter{q}")
                for c in range(1, NC):
                    last = PE.matmul(ps[:, tok(c)], S[:, c - 1, q * P:(q + 1) * P], CT[:, tok(c)], start=True, stop=True)
                sig("ps_inter", last)
                ps = mix_bank(b, f"XT{q}")
                w = slice(q * P, (q + 1) * P)
                sig("ps_XT", mm3(ps[:, :], [(wx_hi[:, w], wx_lo[:, w], xT_hi[:, :], xT_lo[:, :])]))
                wait(PE, "W", b, 2 * q + 2)
                ps = mix_bank(b, f"intra{q}")
                for c in range(NC):
                    for j in range(2):
                        h = 2 * q + j
                        at = (c * 2 + j) * P
                        last = PE.matmul(ps[j * HD:(j + 1) * HD, tok(c)], Xd[:, c, h * HD:(h + 1) * HD],
                                         Wt[:, q % 2, at:at + P], start=True, stop=True)
                sig("ps_intra", last)
            if eng is AC:
                wait(AC, "ps_decb", b, q + 1)
                wait(AC, "skip", b if q else b.prev(), q if q else None)
                sig("decb", AC.copy(decb[:, P:T], bank_of(f"decb{q}")[:, 0:T - P]))
                for f in range(2):
                    u = 2 * q + f
                    wait(AC, "ps_seg", b, u + 1)
                    wait(AC, "ps_st", b)
                    if q >= 2:
                        wait(AC, "ps_intra", b, q - 1)
                    sig("segexp", AC.activation(Wt[:, q % 2, f * T:(f + 1) * T], bank_of(f"seg{u}")[:, :], ACT.Exp))
            if eng is DVE:
                for f in range(2):
                    u = 2 * q + f
                    wait(DVE, "segexp", b, u + 1)
                    wv = Wt[:, q % 2, f * T:(f + 1) * T].rearrange("p (c j t) -> p c j t", c=HF, j=2)
                    sig("W", DVE.tensor_tensor(
                        wv, wv, Gm[:, f * HF:(f + 1) * HF, :].unsqueeze(2).to_broadcast([P, HF, 2, P]), ALU.mult))
                wait(DVE, "ps_inter", b, q + 1)
                wait(DVE, "decb", b, q + 1)
                sig("inter", DVE.tensor_tensor(decb[:, P:T], bank_of(f"inter{q}")[:, P:T], decb[:, P:T], ALU.mult))
                wait(DVE, "ps_XT", b, q + 1)
                wait(DVE, "inter", b, q + 1)
                wait(DVE, "gated", b if q else b.prev(), q if q else None)
                sig("skip", DVE.scalar_tensor_tensor(yt[:, :], bank_of(f"XT{q}")[:, :], d_col[:, q:q + 1], decb[:, :],
                                                     ALU.mult, ALU.add))
                wait(DVE, "ps_intra", b, q + 1)
                wait(DVE, "skip", b, q + 1)
                sig("y", DVE.tensor_tensor(yt[:, :], bank_of(f"intra{q}")[:, :], yt[:, :], ALU.add))
                wait(DVE, "y", b, q + 1)
                wait(DVE, "zg", b, q + 1)
                sig("gated", DVE.tensor_tensor(zg[:, q, :], yt[:, :], zg[:, q, :], ALU.mult))

        def mix_out(eng, b):
            if eng is PE:
                wait(PE, "gated", b)
                ps = mix_bank(b, "out")
                for c in range(NC):
                    for q in range(NQ):
                        last = PE.matmul(ps[:, tok(c)], zg[:, q, tok(c)], wout[:, q, :], start=(q == 0), stop=(q == NQ - 1))
                sig("ps_out", last)
            if eng is DVE:
                wait(DVE, "ps_out", b)
                wait(DVE, "copied", b)
                sig("v", DVE.tensor_tensor(resid[:, :, :], bank_of("out")[:, :].rearrange("p (c d) -> p c d", c=NC),
                                           resid[:, :, :], ALU.add))

        def layer_norm(eng, b, pre, src, dst, done, before_write):
            veps, lnv, r0, t0, t1, rstd = (nrm[:, k, :] for k in range(6))
            if eng is DVE:
                n = [0]
                for c in range(NC):
                    last = DVE.bn_stats(st6[:, c, :], src[:, c, :])
                link(DVE, pre + "_v", b, last, n)
                alone(DVE)
                for c in range(NC):
                    last = DVE.bn_aggr(mv[:, c, :], st6[:, c, :])
                link(DVE, pre + "_v", b, last, n)
                link(DVE, pre + "_v", b, DVE.tensor_scalar(veps, mv[:, :, 1], LN_EPS, None, ALU.add), n)
                wait(DVE, pre + "_s", b)
                link(DVE, pre + "_v", b, DVE.tensor_tensor(t0, r0, r0, ALU.mult), n)
                link(DVE, pre + "_v", b, DVE.tensor_tensor(t1, t0, veps, ALU.mult), n)
                link(DVE, pre + "_v", b, DVE.tensor_scalar(t0, t1, -0.5, 1.5, ALU.mult, ALU.add), n)
                link(DVE, pre + "_v", b, DVE.tensor_tensor(rstd, r0, t0, ALU.mult), n)
                before_write()
                for c in range(NC):
                    last = DVE.tensor_scalar(dst[:, c, :], src[:, c, :], mv[:, c, 0:1], rstd[:, c:c + 1],
                                             ALU.subtract, ALU.mult)
                sig(done, last)
                wait(DVE, done, b)
            if eng is AC:
                wait(AC, pre + "_v", b, 3)
                sig(pre + "_s", AC.activation(lnv, veps, ACT.Ln))
                wait(AC, pre + "_s", b, 1)
                sig(pre + "_s", AC.activation(r0, lnv, ACT.Exp, scale=-0.5))

        def route_norm(eng, b):
            if eng is DVE:
                wait(DVE, "v", b)
            layer_norm(eng, b, "ln1", resid, x1, "x1", lambda: wait(DVE, "o", b.prev()))
            if eng is PE:
                wait(PE, "x1", b)
                wait(PE, "comb", b.prev())
                for c in range(NC):
                    last = PE.transpose(hb[0][:, tok(c)], x1[:, c, :], ident[:, :])
                sig("ps_x1T", last)
            if eng is AC:
                wait(AC, "ps_x1T", b)
                wait(AC, "stored", b.prev())
                sig("x1T", AC.copy(x1T, hb[0][:, :]))

        def route_logits(eng, b):
            if eng is PE:
                wait(PE, "x1T", b)
                for c in range(NC):
                    last = PE.matmul(hb[1][:, tok(c)], x1T[:, tok(c)], router[:, :], start=True, stop=True)
                sig("ps_lg", last)
            if eng is AC:
                wait(AC, "ps_lg", b)
                wait(AC, "gelu_hi", b.prev())
                wait(AC, "gelu_lo", b.prev())
                sig("lg", AC.copy(lg[:, :, :].rearrange("p (c r) e -> p c (r e)", c=NC),
                                  hb[1][:, :].rearrange("p (c n) -> p c n", c=NC)[:, :, 0:NR * E]))

        def route_weights(eng, b):
            NGR = NC * NR
            wide3 = [P, NGR, E]
            if eng is DVE:
                n = [0]
                wait(DVE, "lg", b)
                wait(DVE, "gelu_lo", b.prev())
                alone(DVE)
                for g in range(NGR):
                    last = DVE.max(mx[:, g, :], lg[:, g, :])
                link(DVE, "rt_v", b, last, n)
                alone(DVE)
                for g in range(NGR):
                    last = DVE.max_index(ix[:, g, :], mx[:, g, :], lg[:, g, :])
                link(DVE, "rt_v", b, last, n)
                link(DVE, "rt_v", b, DVE.tensor_tensor(lg[:, :, :], lg[:, :, :], mx[:, :, 0:1].to_broadcast(wide3),
                                                       ALU.subtract), n)
                for k in range(TOPK):
                    last = DVE.tensor_tensor(hot[:, k, :, :], iota_e[:, :].unsqueeze(1).to_broadcast(wide3),
                                             ix[:, :, k:k + 1].to_broadcast(wide3), ALU.is_equal)
                link(DVE, "rt_v", b, last, n)
                link(DVE, "rt_v", b, DVE.tensor_tensor(hot[:, 0], hot[:, 0], hot[:, 1], ALU.add), n)
                link(DVE, "rt_v", b, DVE.tensor_tensor(hot[:, 0], hot[:, 0], hot[:, 2], ALU.add), n)
                wait(DVE, "rt_s", b)
                link(DVE, "rt_v", b, DVE.tensor_tensor(lg[:, :, :], lg[:, :, :], hot[:, 0], ALU.mult), n)
                link(DVE, "rt_v", b, DVE.tensor_reduce(ssum[:, :], lg[:, :, :], AX.X, ALU.add), n)
                wait(DVE, "ps_dwT", b.prev())
                sig("dw", DVE.reciprocal(srec[:, :], ssum[:, :]))
                wait(DVE, "dw", b)
                lv = lg[:, :, :].rearrange("p (c r) e -> p c r e", c=NC)
                rv = srec[:, :].rearrange("p (c r) -> p c r", c=NC)
                for r, dst in ((0, dwpad[:, :, 0:E]), (1, dw2[:, :, :]), (2, dwpad[:, :, B2ROW:B2ROW + E])):
                    last = DVE.tensor_tensor(dst, lv[:, :, r, :], rv[:, :, r:r + 1].to_broadcast([P, NC, E]), ALU.mult)
                sig("dwr", last)
            if eng is AC:
                wait(AC, "rt_v", b, 3)
                sig("rt_s", AC.activation(lg[:, :, :], lg[:, :, :], ACT.Exp))

        def route_rows(eng, b):
            R1 = slice(0, E)
            if eng is PE:
                wait(PE, "dwr", b)
                alone(PE)
                for c in range(NC):
                    last = PE.transpose(hb[2][0:DTROW, tok(c)], dwpad[:, c, :], ident[:, :])
                sig("ps_dwT", last)
            if eng is AC:
                wait(AC, "ps_dwT", b)
                wait(AC, "ps_b2", b.prev())
                sig("dwT", AC.copy(rows[0:DTROW, :], hb[2][0:DTROW, :]))
            if eng is DVE:
                wait(DVE, "dwT", b)
                wait(DVE, "ps_row", b.prev())
                sig("dw_hi", DVE.tensor_copy(rows_hi[R1, :], rows[R1, :]))
                wait(DVE, "dw_hi", b)
                sig("dw_lo", DVE.tensor_tensor(rows_lo[R1, :], rows[R1, :], rows_hi[R1, :].bitcast(F32), ALU.subtract))

        def broadcast_row(b, e):
            wait(PE, "dw_lo", b)
            if e == 0:
                wait(PE, "acc", b.prev())
            else:
                wait(PE, "xw", b, e)
            sel = pick[0:E, e:e + 1].to_broadcast([E, P])
            PE.matmul(rb[:, :], sel, rows_hi[0:E, :], start=True, stop=False)
            sig("ps_row", PE.matmul(rb[:, :], sel, rows_lo[0:E, :], start=False, stop=True))

        def expert_in(eng, b, es):
            for e in es:
                if eng is PE:
                    if e == 0:
                        broadcast_row(b, 0)
                        broadcast_row(b, 1)
                        wait(PE, "x1T", b)
                        wait(PE, "lg", b)
                        wait(PE, "dwT", b)
                    if 2 <= e + 1 < E:
                        broadcast_row(b, e + 1)
                    wait(PE, "xw_lo", b, e + 1)
                    for hc in range(NH):
                        w = slice(hc * P, (hc + 1) * P)
                        last = mm3(hb[hc][:, :], [(w1_hi[:, e, w], w1_lo[:, e, w], sp_hi[:, e % 3, :], sp_lo[:, e % 3, :])],
                                   start=(e == 0), stop=(e == E - 1))
                    sig("ps_h", last)
                if eng is DVE:
                    wait(DVE, "ps_row", b, e + 1)
                    if e >= 2:
                        wait(DVE, "xw_hi", b, e - 1)
                        wait(DVE, "xw_lo", b, e - 1)
                    else:
                        wait(DVE, "gelu_hi", b.prev())
                        wait(DVE, "gelu_lo", b.prev())
                    sig("xw", DVE.tensor_tensor(wide[e % 2], rb[:, :], x1T, ALU.mult))
                if eng is AC:
                    wait(AC, "xw", b, e + 1)
                    if e >= 3:
                        wait(AC, "ps_h", b, e - 2)
                    else:
                        wait(AC, "ps_y", b.prev())
                        if b.reg is not None or b.off < NB - 1:
                            wait(AC, "ps_zg", Batch(b.reg, b.off + 1))
                    sig("xw_hi", AC.copy(sp_hi[:, e % 3, :], wide[e % 2]))
                if eng is PO:
                    wait(PO, "xw_hi", b, e + 1)
                    sig("xw_lo", PO.tensor_tensor(sp_lo[:, e % 3, :], wide[e % 2], sp_hi[:, e % 3, :].bitcast(F32),
                                                  ALU.subtract))

        def expert_gelu(eng, b):
            for k in range(NH):
                g = wide[k % 2]
                if eng is AC:
                    wait(AC, "ps_h", b)
                    if k >= 2:
                        wait(AC, "gelu_hi", b, k - 1)
                        wait(AC, "gelu_lo", b, k - 1)
                    else:
                        wait(AC, "xw_hi", b)
                        wait(AC, "xw_lo", b)
                    sig("gelu", AC.activation(g, hb[k][:, :], ACT.Gelu))
                if eng is DVE:
                    wait(DVE, "ps_h", b)
                    wait(DVE, "gelu", b, k + 1)
                    sig("gelu_hi", DVE.tensor_copy(sp_hi[:, k, :], g))
                if eng is PO:
                    wait(PO, "gelu_hi", b, k + 1)
                    sig("gelu_lo", PO.tensor_tensor(sp_lo[:, k, :], g, sp_hi[:, k, :].bitcast(F32), ALU.subtract))

        def expert_b2(eng, b):
            R = slice(B2ROW, B2ROW + E)
            if eng is PE:
                wait(PE, "xw", b)
                for c in range(NC):
                    last = PE.matmul(rb[:, tok(c)], rows[R, tok(c)], b2_sb[R, :], start=True, stop=True)
                sig("ps_b2", last)
            if eng is DVE:
                wait(DVE, "ps_b2", b)
                wait(DVE, "ps_x1T", b)
                sig("acc", DVE.tensor_tensor(x1, rb[:, :].rearrange("p (c d) -> p c d", c=NC), x1, ALU.add))
                wait(DVE, "acc", b)

        def expert_out(eng, b, c):
            for g in range(NG):
                m = c * NG + g
                if eng is PE:
                    if m == 0:
                        wait(PE, "gelu_lo", b)
                    wait(PE, *(("gelu", b, m + 1) if m < NH else ("comb", b, EG * (m - NH + 1))))
                    w = slice(g * T, (g + 1) * T)
                    sig("ps_y", mm3(hb[m % NH][:, :], [(sp_hi[:, k, tok(c)], sp_lo[:, k, tok(c)], w2_hi[:, k, w], w2_lo[:, k, w])
                                                       for k in range(NH)]))
                if eng is DVE:
                    wait(DVE, "ps_y", b, m + 1)
                    for s in range(EG):
                        e = g * EG + s
                        n = c * E + e
                        if n:
                            wait(DVE, "comb", b, n)
                        sig("comb", DVE.scalar_tensor_tensor(x1[:, c, :], hb[m % NH][:, s * D:(s + 1) * D],
                                                             dw2[:, c, e:e + 1], x1[:, c, :], ALU.mult, ALU.add))

        def expert_norm(eng, b):
            def before_write():
                wait(DVE, "ps_lg", b)
                wait(DVE, "xw", b)
            if eng is DVE:
                wait(DVE, "comb", b)
            layer_norm(eng, b, "ln2", x1, o_sb, "o", before_write)

        def store(eng, b):
            if eng is SP:
                wait(SP, "o", b)
                sig("stored", SP.dma_start(out_rows(b), o_sb))

        def front(eng, b):
            mix_x(eng, b)
            mix_dt(eng, b)
            mix_bc(eng, b)

        def body(eng, b, front_next):
            p = b.prev()
            mix_z(eng, b)
            mix_X(eng, b)
            route_norm(eng, p)
            mix_zg(eng, b)
            route_logits(eng, p)
            mix_keep_x(eng, b)
            if front_next:
                mix_load_next(eng, b)
            mix_scores(eng, b)
            route_weights(eng, p)
            mix_states(eng, b)
            route_rows(eng, p)
            for q in range(NQ):
                expert_in(eng, p, range(q * EX, (q + 1) * EX))
                mix_pair(eng, b, q)
            mix_out(eng, b)
            expert_gelu(eng, p)
            expert_b2(eng, p)
            expert_out(eng, p, 0)
            if front_next:
                front(eng, Batch(b.reg, b.off + 1))
            for c in range(1, NC):
                expert_out(eng, p, c)
            expert_norm(eng, p)
            store(eng, p)

        EX = E // NQ

        def mixer_alone(eng, b):
            front(eng, b)
            mix_z(eng, b)
            mix_X(eng, b)
            split_expert_weights(eng, range(0, 4))
            mix_zg(eng, b)
            mix_keep_x(eng, b)
            mix_load_next(eng, b)
            split_expert_weights(eng, range(4, 8))
            mix_scores(eng, b)
            mix_states(eng, b)
            for q in range(NQ):
                mix_pair(eng, b, q)
                split_expert_weights(eng, range(8 + 4 * q, 12 + 4 * q))
            mix_out(eng, b)

        def mixture_alone(eng, b):
            route_norm(eng, b)
            route_logits(eng, b)
            route_weights(eng, b)
            route_rows(eng, b)
            expert_in(eng, b, range(E))
            expert_gelu(eng, b)
            expert_b2(eng, b)
            for c in range(NC):
                expert_out(eng, b, c)
            expert_norm(eng, b)
            store(eng, b)

        def program(eng):
            waited[id(eng)] = {}
            setup(eng)
            mixer_alone(eng, Batch(None, 0))
            front(eng, Batch(None, 1))
            expert_weights_ready(eng)
            body(eng, Batch(None, 1), True)
            waited[id(eng)] = {}
            with eng.Fori(2, NB - 1) as i:
                body(eng, Batch(i, 0), True)
            waited[id(eng)] = {}
            body(eng, Batch(None, NB - 1), False)
            mixture_alone(eng, Batch(None, NB - 1))
            if eng is SP:
                wait(SP, "stored", Batch(None, NB - 1))

        product("dwr", 1)
        block = ctx.enter_context(nc.Block())

        @block.sync
        def _(eng):
            program(SP)

        @block.tensor
        def _(eng):
            program(PE)

        @block.vector
        def _(eng):
            program(DVE)

        @block.scalar
        def _(eng):
            program(AC)

        @block.gpsimd
        def _(eng):
            program(PO)

        for p in prods.values():
            written = 3 if p.name != "x_in" else 2
            assert p.done % p.n == 0 and p.done // p.n >= written - 1, (p.name, p.done, p.n)


def kernel(L0_attn_x, L0_attn_Wz, L0_attn_Win, L0_attn_Wzg, L0_attn_Wout, L0_attn_dt_bias, L0_attn_A_log,
           L0_attn_D_param, L0_ffn_P_w, L0_ffn_U1, L0_ffn_U2, L0_ffn_U3, L0_ffn_W1, L0_ffn_W2, L0_ffn_b2):
    import concourse.bacc as bacc
    from concourse.bass_utils import run_bass_kernel_spmd

    lay = np.ascontiguousarray
    w2 = np.asarray(L0_ffn_W2)
    arrays = dict(
        x=lay(L0_attn_x), Wz=lay(L0_attn_Wz), Win=lay(L0_attn_Win), Wzg=lay(L0_attn_Wzg), Wout=lay(L0_attn_Wout),
        dt_bias=lay(L0_attn_dt_bias), A_log=lay(L0_attn_A_log), D_param=lay(L0_attn_D_param), P_w=lay(L0_ffn_P_w),
        U1T=lay(np.asarray(L0_ffn_U1).T), U2T=lay(np.asarray(L0_ffn_U2).T), U3T=lay(np.asarray(L0_ffn_U3).T),
        W1T=lay(np.asarray(L0_ffn_W1).transpose(2, 0, 1)),
        W2T=lay(w2.transpose(2, 0, 1).reshape(w2.shape[2], -1)),
        b2=lay(L0_ffn_b2),
    )
    nc = bacc.Bacc("TRN2", target_bir_lowering=False, num_devices=1)
    aps = [nc.dram_tensor("in_" + k, v.shape, mybir.dt.from_np(v.dtype), kind="ExternalInput").ap() for k, v in arrays.items()]
    res = nc.dram_tensor("result", (NB, T, D), F32, kind="ExternalOutput").ap()
    layer_program(nc, *aps, res)
    r = run_bass_kernel_spmd(nc, [{"in_" + k: v for k, v in arrays.items()}], core_ids=[0])
    return r.results[0]["result"]
```

```python
from contextlib import ExitStack

import numpy as np

import concourse.bass as bass
from concourse import mybir

F32 = mybir.dt.float32
F32R = mybir.dt.float32r
I32 = mybir.dt.int32
U32 = mybir.dt.uint32
ALU = mybir.AluOpType
ACT = mybir.ActivationFunctionType
AX = mybir.AxisListType

P = 128
D = 128
NB, T = 16, 512
NC = T // P
H, HD, NS = 8, 64, 64
NQ = H // 2
DI = H * HD
DZ = 2 * D
NK = DZ // P
E, TOPK = 12, 3
HID = 512
NH = HID // P
NG = E * D // T
EG = E // NG
NR = 3
B2ROW = 32
DTROW = 64
LN_EPS = 1e-5

MIX_USES = (
    [("xT", "xT", 1), ("dtB", "dt_raw", 1), ("BC", "BC", 1)]
    + [(f"z{k}", "silu", k + 1) for k in range(NK)]
    + [(f"X{c}", "Xd", c + 1) for c in range(NC)]
    + [(f"zg{q}", "zg", q + 1) for q in range(NQ)]
    + [("G", "Gm", 1), ("cum", "cumexp", 1), ("ends", "ends", 1)]
    + [(f"st{c}", "state", c + 1) for c in range(NC - 1)]
    + [u for q in range(NQ) for u in (
        (f"seg{2 * q}", "segexp", 2 * q + 1), (f"seg{2 * q + 1}", "segexp", 2 * q + 2), (f"decb{q}", "decb", q + 1),
        (f"inter{q}", "inter", q + 1), (f"XT{q}", "skip", q + 1), (f"intra{q}", "y", q + 1))]
    + [("out", "v", 1)]
)
MIX_USE = {u[0]: n for n, u in enumerate(MIX_USES)}
NX = 3


class Batch:

    def __init__(self, reg, off):
        self.reg, self.off = reg, off

    def prev(self):
        return Batch(self.reg, self.off - 1)

    def index(self):
        if self.reg is None:
            return self.off
        return self.reg + self.off if self.off else self.reg


class Product:

    def __init__(self, sem, name, n, step=1):
        self.sem, self.name, self.n, self.step = sem, name, n, step
        self.done = 0


def layer_program(nc, x, Wz, Win, Wzg, Wout, dt_bias, A_log, D_param, P_w, U1T, U2T, U3T, W1T, W2T, b2, out):
    ctx = ExitStack()
    with ctx:
        def sb(name, shape, dt=F32):
            return ctx.enter_context(nc.sbuf_tensor(name, shape, dt))

        w1_hi, w1_lo = sb("w1_hi", [P, E, HID], F32R), sb("w1_lo", [P, E, HID], F32R)
        w2_hi, w2_lo = sb("w2_hi", [P, NH, E * D], F32R), sb("w2_lo", [P, NH, E * D], F32R)
        wbc_hi, wbc_lo = sb("wbc_hi", [P, 2 * NS], F32R), sb("wbc_lo", [P, 2 * NS], F32R)
        wz_hi, wz_lo = sb("wz_hi", [P, DZ], F32R), sb("wz_lo", [P, DZ], F32R)
        wx_hi, wx_lo = sb("wx_hi", [P, DI], F32R), sb("wx_lo", [P, DI], F32R)
        wzg_hi, wzg_lo = sb("wzg_hi", [P, NK, DI], F32R), sb("wzg_lo", [P, NK, DI], F32R)
        wbdt = sb("wbdt", [P, P])
        wout = sb("wout", [P, NQ, D])
        router = sb("router", [P, P])
        b2_sb = sb("b2_sb", [NS, D])
        ident, upper = sb("ident", [P, P]), sb("upper", [P, P])
        strict_r = sb("strict_r", [P, P], F32R)
        pick_f, pick = sb("pick_f", [P, E]), sb("pick", [P, E], F32R)
        pairs = sb("pairs", [P, DI], F32R)
        iota_i, iota_e = sb("iota_i", [P, E], I32), sb("iota_e", [P, E])
        bias_b, neg_a, d_col = sb("bias_b", [P, H]), sb("neg_a", [P, H]), sb("d_col", [P, NQ])
        x_in = sb("x_in", [P, NC, D])
        xT = sb("xT", [P, T])
        xT_hi, xT_lo = sb("xT_hi", [P, T], F32R), sb("xT_lo", [P, T], F32R)
        BT, CT = sb("BT", [NS, T]), sb("CT", [NS, T])
        B_tok = sb("B_tok", [P, NC, NS])
        Xd = sb("Xd", [P, NC, DI])
        Ua_hi, Ua_lo = sb("Ua_hi", [P, T], F32R), sb("Ua_lo", [P, T], F32R)
        Gm = sb("Gm", [P, NC, P])
        Wt = sb("Wt", [P, 2, 2 * T])
        S = sb("S", [NS, NC - 1, DI])
        pw, ut = S[:, 0, 0:D], S[:, 0, D:2 * D]
        decb = sb("decb", [P, T])
        yt = sb("yt", [P, T])
        zg = sb("zg", [P, NQ, T])
        dt_s = sb("dt_s", [P, 6, NC * H])
        delta, a = sb("delta", [P, NC, H]), sb("a", [P, NC, H])
        a_hi, a_lo = sb("a_hi", [P, NC, H], F32R), sb("a_lo", [P, NC, H], F32R)
        ends = sb("ends", [P, (NC - 1) * H])
        total = sb("total", [NS, NC * H])
        silu = Wt[:, 0, :].rearrange("p (k t) -> p k t", k=NK)
        pairs_f = Wt[:, 1, 0:DI]
        strict = Wt[:, 0, 0:P]
        Xde = Wt[:, :, :].rearrange("p a b -> p (a b)")[:, 0:(NC - 1) * DI].rearrange("p (c n) -> p c n", c=NC - 1)
        rows = sb("rows", [P, T])
        rows_hi, rows_lo = sb("rows_hi", [P, T], F32R), sb("rows_lo", [P, T], F32R)
        fbuf = sb("fbuf", [P, 4, T])
        x1 = fbuf[:, 0, :].rearrange("p (c d) -> p c d", c=NC)
        x1T = fbuf[:, 1, :]
        acc = sb("acc", [P, NC, D])
        acc_odd = sb("acc_odd", [P, D])
        wide = [fbuf[:, 2, :], fbuf[:, 3, :]]
        sp_hi, sp_lo = sb("sp_hi", [P, NH, T], F32R), sb("sp_lo", [P, NH, T], F32R)
        lg = fbuf[:, 3, 0:NC * NR * E].rearrange("p (g e) -> p g e", e=E)
        mx = fbuf[:, 3, NC * NR * E:NC * NR * (E + 8)].rearrange("p (g e) -> p g e", e=8)
        ix = sb("ix", [P, NC * NR, 8], U32)
        hot = fbuf[:, 2, 0:TOPK * NC * NR * E].rearrange("p (k g e) -> p k g e", k=TOPK, g=NC * NR)
        ssum, srec = sb("ssum", [P, NC * NR]), sb("srec", [P, NC * NR])
        dw2_new, dw2 = sb("dw2_new", [P, NC, E]), sb("dw2", [P, NC, E])
        dwpad = sb("dwpad", [P, NC, DTROW])
        st6, mv, nrm = sb("st6", [P, NC, 6]), sb("mv", [P, NC, 2]), sb("nrm", [P, 6, NC])

        xb = [ctx.enter_context(nc.psum_tensor(f"mix_bank{n}", [P, T], F32)) for n in range(NX)]
        hb = [ctx.enter_context(nc.psum_tensor(f"exp_bank{n}", [P, T], F32)) for n in range(NH)]
        rb = ctx.enter_context(nc.psum_tensor("row_bank", [P, T], F32))

        prods = {}

        def product(name, n, step=1):
            prods[name] = Product(ctx.enter_context(nc.semaphore(name)), name, n, step)

        for name, n in dict(
            ps_xT=1, xT=1, xT_lo=1, ps_dtB=1, B_tok=1, dt_raw=1, dt_v=13, dt_s=2, a_split=2, ps_BC=1, BC=1,
            ps_z=NK, tanh=NK, silu=NK, silu_hi=NK, silu_lo=NK, ps_X=NC, Xd=NC, ps_zg=NQ, zg=NQ,
            ps_G=1, Gm=1, ps_cum=1, cumexp=1, cum_hi=1, cum_lo=1, ps_ends=1, ends=1, Xde=NC - 1,
            ps_st=NC - 1, state=NC - 1, st_tmp=NC - 2, ps_decb=NQ, decb=NQ, Ua=2 * NQ, ps_seg=2 * NQ, segexp=2 * NQ,
            W=2 * NQ, ps_inter=NQ, inter=NQ, ps_XT=NQ, skip=NQ, ps_intra=NQ, y=NQ, gated=NQ, ps_out=1, v=1,
            ln1_v=7, ln1_s=2, x1=1, ps_x1T=1, x1T=1, ps_lg=1, lg=1, rt_v=8, rt_s=1, dw=1, ps_dwT=1, dwT=1, dw_hi=1,
            dw_lo=1, ps_row=E, xw=E, xw_hi=E, xw_lo=E, ps_h=E, gelu=NH, gelu_hi=NH, gelu_lo=NH, ps_b2=1, acc=1, 
            ps_y=NC * NG, comb=NC * (E + 1), ln2_v=7, ln2_s=2, o=1,
        ).items():
            product(name, n)
        product("x_in", 1, 16)
        product("stored", 1, 16)
        sems = {n: ctx.enter_context(nc.semaphore("set_" + n)) for n in
                ("mix_w", "small", "ring0", "ring1", "ring2", "ring3", "w_hi", "w_lo", "masks", "cast", "chain", "alog", "ps_r", "router", "pad")}

        waited = {}

        def wait(eng, name, b, k=None):
            p = prods[name]
            v = b.off * p.n * p.step + (p.n if k is None else k) * p.step
            seen = waited.setdefault(id(eng), {})
            if (b.reg is None and v <= 0) or seen.get(name, -10**9) >= v:
                return
            seen[name] = v
            eng.wait_ge(p.sem, v if b.reg is None else b.reg * (p.n * p.step) + v)

        def alone(eng):
            eng.nop(nofuse=True)

        def sig(name, ins):
            p = prods[name]
            p.done += 1
            ins.then_inc(p.sem, p.step)

        def link(eng, name, b, ins, count):
            count[0] += 1
            sig(name, ins)
            wait(eng, name, b, count[0])

        def mm3(ps, pairs, start=True, stop=True):
            last = None
            n = len(pairs)
            for j, (s_hi, s_lo, m_hi, m_lo) in enumerate(pairs):
                nc.tensor.matmul(ps, s_hi, m_hi, start=start and j == 0, stop=False)
                nc.tensor.matmul(ps, s_hi, m_lo, start=False, stop=False)
                last = nc.tensor.matmul(ps, s_lo, m_hi, start=False, stop=stop and j == n - 1)
            return last

        def mix_bank(b, use):
            n = MIX_USE[use]
            if n >= NX:
                before, owner = n - NX, b
            else:
                before, owner = max(m for m in range(len(MIX_USES)) if m % NX == n), b.prev()
            _, reader, k = MIX_USES[before]
            wait(nc.tensor, reader, owner, k)
            return xb[n % NX]

        def bank_of(use):
            return xb[MIX_USE[use] % NX]

        tok = lambda c: slice(c * P, (c + 1) * P)
        PE, DVE, AC, PO, SP = nc.tensor, nc.vector, nc.scalar, nc.gpsimd, nc.sync

        NW = 2 * E
        RING = 4
        mix_stage = Xd[:, :, :].rearrange("p c n -> p (c n)")
        st_win, st_wz = mix_stage[:, 0:648], mix_stage[:, 648:904]
        st_wzg = mix_stage[:, 904:904 + NK * DI].rearrange("p (k n) -> p k n", k=NK)

        def w_tile(k):
            if k < E:
                return W1T[:, k, :], w1_hi[:, k, :], w1_lo[:, k, :]
            kc, g = divmod(k - E, NG)
            cols = slice(g * T, (g + 1) * T)
            return W2T[kc * P:(kc + 1) * P, cols], w2_hi[:, kc, cols], w2_lo[:, kc, cols]

        def setup(eng):
            if eng is SP:
                SP.dma_start(x_in[:, :, :], x[0].rearrange("(c p) d -> p c d", p=P)).then_inc(prods["x_in"].sem, 16)
                SP.dma_start(st_win, Win[:, :]).then_inc(sems["mix_w"], 16)
                SP.dma_start(st_wz, Wz[:, :]).then_inc(sems["mix_w"], 16)
                SP.dma_start(st_wzg, Wzg.rearrange("(k p) n -> p k n", p=P)).then_inc(sems["mix_w"], 16)
                SP.wait_ge(sems["pad"], 2)
                SP.dma_start(wbdt[:, 0:NS], Win[:, 0:NS]).then_inc(sems["small"], 16)
                SP.dma_start(wbdt[:, NS:NS + H], Win[:, 2 * NS:2 * NS + H]).then_inc(sems["small"], 16)
                SP.dma_start(bias_b[:, :], dt_bias.partition_broadcast(P)).then_inc(sems["small"], 16)
                SP.dma_start(neg_a[:, :], A_log.partition_broadcast(P)).then_inc(sems["small"], 16)
                for j in range(2):
                    SP.dma_start(d_col[j * HD:(j + 1) * HD, :],
                                 D_param.rearrange("(q j) -> j q", j=2)[j, :].partition_broadcast(HD),
                                 allow_slow_non_contiguous=True).then_inc(sems["small"], 16)
                SP.dma_start(wout[:, :, :], Wout.rearrange("(q p) n -> p q n", p=P)).then_inc(sems["small"], 16)
                SP.dma_start(pw, P_w[:, :]).then_inc(sems["small"], 16)
                for r, u in enumerate((U1T, U2T, U3T)):
                    SP.dma_start(ut[:, r * E:(r + 1) * E], u[:, :]).then_inc(sems["small"], 16)
                SP.dma_start(b2_sb[B2ROW:B2ROW + E, :], b2[:, :]).then_inc(sems["small"], 16)
                for k in range(NW):
                    if k >= RING:
                        SP.wait_ge(sems["w_hi"], k - RING + 1)
                        SP.wait_ge(sems["w_lo"], k - RING + 1)
                        SP.wait_ge(sems[f"ring{k % RING}"], 16 * (k // RING))
                    SP.dma_start(fbuf[:, k % RING, :], w_tile(k)[0]).then_inc(sems[f"ring{k % RING}"], 16)
            if eng is PO:
                PO.memset(wbdt[:, :], 0.0).then_inc(sems["pad"], 1)
                PO.memset(ut, 0.0).then_inc(sems["pad"], 1)
                for m, v in ((ident[:, :], 0.0), (upper[:, :], 1.0), (strict, 1.0)):
                    PO.memset(m, v).then_inc(sems["masks"], 1)
                PO.memset(pick_f[:, :], 0.0).then_inc(sems["masks"], 1)
                PO.memset(pairs_f, 0.0).then_inc(sems["masks"], 1)
                PO.memset(dwpad[:, :, :], 0.0).then_inc(sems["masks"], 1)
                PO.memset(decb[:, 0:P], 0.0).then_inc(sems["masks"], 1)
                PO.iota(iota_i[:, :], pattern=[[1, E]], base=0, channel_multiplier=0).then_inc(sems["masks"], 1)
                PO.wait_ge(sems["masks"], 8)
                PO.affine_select(out=ident[:, :], in_=ident[:, :], compare_op=ALU.not_equal, fill=1.0, base=0,
                                 pattern=[[-1, P]], channel_multiplier=1).then_inc(sems["masks"], 1)
                PO.affine_select(out=upper[:, :], in_=upper[:, :], compare_op=ALU.is_ge, fill=0.0, base=0,
                                 pattern=[[1, P]], channel_multiplier=-1).then_inc(sems["masks"], 1)
                PO.affine_select(out=strict, in_=strict, compare_op=ALU.is_gt, fill=0.0, base=0,
                                 pattern=[[-1, P]], channel_multiplier=1).then_inc(sems["masks"], 1)
                PO.affine_select(out=pick_f[:, :], in_=pick_f[:, :], compare_op=ALU.not_equal, fill=1.0, base=0,
                                 pattern=[[-1, E]], channel_multiplier=1).then_inc(sems["masks"], 1)
                PO.affine_select(out=pairs_f, in_=pairs_f, compare_op=ALU.not_equal, fill=1.0, base=-DTROW,
                                 pattern=[[-1, H], [0, HD]], channel_multiplier=1).then_inc(sems["masks"], 1)
            if eng is DVE:
                DVE.wait_ge(sems["mix_w"], 48)
                DVE.tensor_scalar(st_wzg, st_wzg, 0.5, None, ALU.mult).then_inc(sems["chain"], 1)
                DVE.wait_ge(sems["chain"], 1)
                parts = ((st_win[:, 0:2 * NS], wbc_hi[:, :], wbc_lo[:, :]), (st_wz, wz_hi[:, :], wz_lo[:, :]),
                         (st_win[:, 2 * NS + H:], wx_hi[:, :], wx_lo[:, :]),
                         (st_wzg, wzg_hi[:, :, :], wzg_lo[:, :, :]))
                for src, hi, _ in parts:
                    last = DVE.tensor_copy(hi, src)
                last.then_inc(sems["chain"], 1)
                DVE.wait_ge(sems["chain"], 2)
                for src, hi, lo in parts:
                    DVE.tensor_tensor(lo, src, hi.bitcast(F32), ALU.subtract).then_inc(sems["cast"], 1)
                DVE.wait_ge(sems["masks"], 13)
                DVE.tensor_copy(strict_r[:, :], strict).then_inc(sems["cast"], 1)
                DVE.tensor_copy(pick[:, :], pick_f[:, :]).then_inc(sems["cast"], 1)
                DVE.tensor_copy(pairs[:, :], pairs_f).then_inc(sems["cast"], 1)
                DVE.tensor_copy(iota_e[:, :], iota_i[:, :]).then_inc(sems["cast"], 1)
                DVE.wait_ge(sems["cast"], 8)
                DVE.wait_ge(sems["alog"], 1)
                DVE.tensor_scalar(neg_a[:, :], neg_a[:, :], -1.0, None, ALU.mult).then_inc(sems["chain"], 1)
                DVE.wait_ge(sems["chain"], 3)
                DVE.wait_ge(sems["ps_r"], 1)
                DVE.tensor_copy(router[:, :], rb[:, 0:P]).then_inc(sems["router"], 1)
            if eng is AC:
                AC.wait_ge(sems["small"], 16 * 12)
                AC.activation(neg_a[:, :], neg_a[:, :], ACT.Exp).then_inc(sems["alog"], 1)
            if eng is PE:
                PE.wait_ge(sems["small"], 16 * 12)
                PE.wait_ge(sems["masks"], 13)
                PE.wait_ge(sems["pad"], 2)
                PE.matmul(rb[:, 0:P], pw, ut, start=True, stop=True).then_inc(sems["ps_r"], 1)
                PE.wait_ge(sems["cast"], 8)

        def split_expert_weights(eng, ks):
            for k in ks:
                _, hi, lo = w_tile(k)
                if eng is AC:
                    AC.wait_ge(sems[f"ring{k % RING}"], 16 * (k // RING + 1))
                    AC.copy(hi, fbuf[:, k % RING, :]).then_inc(sems["w_hi"], 1)
                if eng is PO:
                    PO.wait_ge(sems["w_hi"], k + 1)
                    PO.tensor_tensor(lo, fbuf[:, k % RING, :], hi.bitcast(F32), ALU.subtract).then_inc(sems["w_lo"], 1)

        def expert_weights_ready(eng):
            if eng in (PE, DVE, AC):
                eng.wait_ge(sems["w_lo"], NW)
                eng.wait_ge(sems["w_hi"], NW)
            if eng is PE:
                eng.wait_ge(sems["router"], 1)

        def mix_x(eng, b):
            if eng is PE:
                wait(PE, "x_in", b)
                ps = mix_bank(b, "xT")
                for c in range(NC):
                    last = PE.transpose(ps[:, tok(c)], x_in[:, c, :], ident[:, :])
                sig("ps_xT", last)
            if eng is AC:
                wait(AC, "ps_xT", b)
                wait(AC, "ps_XT", b.prev())
                AC.copy(xT_hi[:, :], bank_of("xT")[:, :])
                sig("xT", AC.copy(xT[:, :], bank_of("xT")[:, :]))
            if eng is DVE:
                wait(DVE, "xT", b)
                wait(DVE, "ps_XT", b.prev())
                sig("xT_lo", DVE.tensor_tensor(xT_lo[:, :], xT[:, :], xT_hi[:, :].bitcast(F32), ALU.subtract))

        def mix_dt(eng, b):
            if eng is PE:
                wait(PE, "xT", b)
                ps = mix_bank(b, "dtB")
                for c in range(NC):
                    last = PE.matmul(ps[:, tok(c)], xT[:, tok(c)], wbdt[:, :], start=True, stop=True)
                sig("ps_dtB", last)
            ps = bank_of("dtB")[:, :].rearrange("p (c n) -> p c n", c=NC)
            e, u, den, one, m, q = (dt_s[:, n, :] for n in range(6))
            if eng is AC:
                wait(AC, "ps_dtB", b)
                wait(AC, "ps_st", b.prev())
                sig("B_tok", AC.copy(B_tok[:, :, :], ps[:, :, 0:NS]))
                wait(AC, "dt_v", b, 1)
                sig("dt_s", AC.activation(e, e, ACT.Exp))
                wait(AC, "dt_v", b, 2)
                sig("dt_s", AC.activation(m, u, ACT.Ln))
            if eng is DVE:
                wait(DVE, "ps_dtB", b)
                wait(DVE, "B_tok", b)
                n = [0]
                flat = delta[:, :, :].rearrange("p c h -> p (c h)")
                wait(DVE, "Xd", b.prev())
                sig("dt_raw", DVE.tensor_tensor(delta[:, :, :], ps[:, :, NS:NS + H],
                                                bias_b[:, :].unsqueeze(1).to_broadcast([P, NC, H]), ALU.add))
                wait(DVE, "dt_raw", b)
                link(DVE, "dt_v", b, DVE.scalar_tensor_tensor(e, flat, -1.0, flat, ALU.mult, ALU.min), n)
                wait(DVE, "dt_s", b, 1)
                link(DVE, "dt_v", b, DVE.tensor_scalar(u, e, 1.0, None, ALU.add), n)
                link(DVE, "dt_v", b, DVE.tensor_scalar(den, u, -1.0, None, ALU.add), n)
                link(DVE, "dt_v", b, DVE.tensor_scalar(one, den, 0.0, None, ALU.is_equal), n)
                link(DVE, "dt_v", b, DVE.tensor_tensor(den, den, one, ALU.add), n)
                link(DVE, "dt_v", b, DVE.reciprocal(q, den), n)
                link(DVE, "dt_v", b, DVE.tensor_tensor(q, q, e, ALU.mult), n)
                wait(DVE, "dt_s", b, 2)
                link(DVE, "dt_v", b, DVE.tensor_tensor(q, q, m, ALU.mult), n)
                link(DVE, "dt_v", b, DVE.tensor_tensor(one, one, e, ALU.mult), n)
                link(DVE, "dt_v", b, DVE.tensor_tensor(q, q, one, ALU.add), n)
                link(DVE, "dt_v", b, DVE.scalar_tensor_tensor(flat, flat, 0.0, q, ALU.max, ALU.add), n)
                wait(DVE, "ps_ends", b.prev())
                wait(DVE, "Ua", b.prev())
                link(DVE, "dt_v", b, DVE.tensor_tensor(
                    a[:, :, :], delta[:, :, :], neg_a[:, :].unsqueeze(1).to_broadcast([P, NC, H]), ALU.mult), n)
                link(DVE, "dt_v", b, DVE.tensor_copy(a_hi[:, :, :], a[:, :, :]), n)
                n2 = [0]
                link(DVE, "a_split", b, DVE.tensor_tensor(
                    a_lo[:, :, :], a[:, :, :], a_hi[:, :, :].bitcast(F32), ALU.subtract), n2)
                link(DVE, "a_split", b, DVE.tensor_copy(dt_s[:, 0, 0:1], dt_s[:, 0, 0:1]), n2)

        def mix_bc(eng, b):
            if eng is PE:
                wait(PE, "xT_lo", b)
                ps = mix_bank(b, "BC")
                sig("ps_BC", mm3(ps[:, :], [(wbc_hi[:, :], wbc_lo[:, :], xT_hi[:, :], xT_lo[:, :])]))
            if eng is AC:
                wait(AC, "ps_BC", b)
                wait(AC, "ps_G", b.prev())
                wait(AC, "ps_inter", b.prev())
                AC.copy(BT[:, :], bank_of("BC")[0:NS, :])
                sig("BC", AC.copy(CT[:, :], bank_of("BC")[NS:2 * NS, :]))

        def mix_load_next(eng, b):
            if eng is SP:
                wait(SP, "ps_xT", b)
                wait(SP, "x1", b)
                sig("x_in", SP.dma_start(x_in[:, :, :], x_rows(Batch(b.reg, b.off + 1))))

        def x_rows(b):
            return x[b.index()].rearrange("(c p) d -> p c d", p=P) if b.reg is None else \
                x[bass.ds(b.index(), 1), :, :].rearrange("o (c p) d -> p (o c) d", p=P)

        def out_rows(b):
            return out[b.index()].rearrange("(c p) d -> p c d", p=P) if b.reg is None else \
                out[bass.ds(b.index(), 1), :, :].rearrange("o (c p) d -> p (o c) d", p=P)

        def mix_z(eng, b):
            for k in range(NK):
                if eng is PE:
                    wait(PE, "xT_lo", b)
                    ps = mix_bank(b, f"z{k}")
                    w = slice(k * P, (k + 1) * P)
                    sig("ps_z", mm3(ps[:, :], [(wz_hi[:, w], wz_lo[:, w], xT_hi[:, :], xT_lo[:, :])]))
                if eng is AC:
                    wait(AC, "ps_z", b, k + 1)
                    wait(AC, "ps_intra", b.prev())
                    sig("tanh", AC.activation(silu[:, k, :], bank_of(f"z{k}")[:, :], ACT.Tanh, scale=0.5))
                if eng is DVE:
                    wait(DVE, "tanh", b, k + 1)
                    sig("silu", DVE.scalar_tensor_tensor(silu[:, k, :], silu[:, k, :], 1.0, bank_of(f"z{k}")[:, :],
                                                         ALU.add, ALU.mult))

        def mix_silu_split(eng, b):
            for k in range(NK):
                if eng is DVE:
                    wait(DVE, "silu", b, k + 1)
                    wait(DVE, "ps_y", b.prev().prev())
                    sig("silu_hi", DVE.tensor_copy(sp_hi[:, k, :], silu[:, k, :]))
                if eng is PO:
                    wait(PO, "silu_hi", b, k + 1)
                    sig("silu_lo", PO.tensor_tensor(sp_lo[:, k, :], silu[:, k, :], sp_hi[:, k, :].bitcast(F32),
                                                    ALU.subtract))

        def mix_X(eng, b):
            for c in range(NC):
                if eng is PE:
                    ps = mix_bank(b, f"X{c}")
                    sig("ps_X", mm3(ps[:, :], [(xT_hi[:, tok(c)], xT_lo[:, tok(c)], wx_hi[:, :], wx_lo[:, :])]))
                if eng is DVE:
                    wait(DVE, "ps_X", b, c + 1)
                    wait(DVE, "ps_intra", b.prev())
                    wait(DVE, "a_split", b)
                    sig("Xd", DVE.tensor_tensor(
                        Xd[:, c, :].rearrange("p (h n) -> p h n", h=H),
                        bank_of(f"X{c}")[:, :].rearrange("p (h n) -> p h n", h=H),
                        delta[:, c, :].unsqueeze(2).to_broadcast([P, H, HD]), ALU.mult))

        def mix_zg(eng, b):
            for q in range(NQ):
                if eng is PE:
                    wait(PE, "silu_lo", b)
                    ps = mix_bank(b, f"zg{q}")
                    w = slice(q * P, (q + 1) * P)
                    sig("ps_zg", mm3(ps[:, :], [(wzg_hi[:, k, w], wzg_lo[:, k, w], sp_hi[:, k, :], sp_lo[:, k, :])
                                                for k in range(NK)]))
                if eng is AC:
                    wait(AC, "ps_zg", b, q + 1)
                    wait(AC, "ps_out", b.prev())
                    sig("zg", AC.copy(zg[:, q, :], bank_of(f"zg{q}")[:, :]))

        def mix_scores(eng, b):
            if eng is PE:
                wait(PE, "BC", b)
                ps = mix_bank(b, "G")
                for c in range(NC):
                    last = PE.matmul(ps[:, tok(c)], BT[:, tok(c)], CT[:, tok(c)], start=True, stop=True)
                sig("ps_G", last)
                wait(PE, "a_split", b)
                ps = mix_bank(b, "cum")
                for c in range(1, NC):
                    last = PE.matmul(ps[DTROW:DTROW + H, tok(c - 1)], a[:, c, :], upper[:, :], start=True, stop=True)
                sig("ps_cum", last)
                ps = mix_bank(b, "ends")
                for part, first in ((a_hi, True), (a_lo, False)):
                    PE.matmul(ps[:, 0:(NC - 1) * H], strict_r[:, :], part[:, 0:NC - 1, :].rearrange("p c h -> p (c h)"),
                              start=first, stop=not first)
                sig("ps_ends", PE.matmul(ps[0:NS, 64:64 + NC * H], upper[:, P - 1:P].to_broadcast([P, NS]), a[:, :, :].rearrange("p c h -> p (c h)"),
                                         start=True, stop=True))
            R = slice(DTROW, DTROW + H)
            cols = (NC - 1) * P
            if eng is DVE:
                wait(DVE, "ps_G", b)
                wait(DVE, "W", b.prev())
                sig("Gm", DVE.tensor_tensor(Gm[:, :, :], bank_of("G")[:, :].rearrange("p (c t) -> p c t", c=NC),
                                            upper[:, :].unsqueeze(1).to_broadcast([P, NC, P]), ALU.mult))
                wait(DVE, "cumexp", b)
                wait(DVE, "ps_decb", b.prev())
                sig("cum_hi", DVE.tensor_copy(rows_hi[R, 0:cols], rows[R, 0:cols]))
                wait(DVE, "cum_hi", b)
                sig("cum_lo", DVE.tensor_tensor(rows_lo[R, 0:cols], rows[R, 0:cols], rows_hi[R, 0:cols].bitcast(F32),
                                                ALU.subtract))
            if eng is AC:
                wait(AC, "ps_cum", b)
                wait(AC, "cum_lo", b.prev())
                sig("cumexp", AC.activation(rows[R, 0:cols], bank_of("cum")[R, 0:cols], ACT.Exp))
                wait(AC, "ps_ends", b)
                wait(AC, "Xde", b.prev())
                wait(AC, "state", b.prev())
                AC.activation(ends[:, :], bank_of("ends")[:, 0:(NC - 1) * H], ACT.Exp)
                sig("ends", AC.activation(total[:, :], bank_of("ends")[0:NS, 64:64 + NC * H], ACT.Exp))
            if eng is PO:
                for c in range(NC - 1):
                    wait(PO, "ends", b)
                    wait(PO, "Xd", b, c + 1)
                    wait(PO, "silu_lo", b)
                    sig("Xde", PO.tensor_tensor(
                        Xde[:, c, :].rearrange("p (h n) -> p h n", h=H), Xd[:, c, :].rearrange("p (h n) -> p h n", h=H),
                        ends[:, c * H:(c + 1) * H].unsqueeze(2).to_broadcast([P, H, HD]), ALU.mult))

        def mix_states(eng, b):
            for c in range(NC - 1):
                if eng is PE:
                    wait(PE, "Xde", b, c + 1)
                    ps = mix_bank(b, f"st{c}")
                    sig("ps_st", PE.matmul(ps[0:NS, :], B_tok[:, c, :], Xde[:, c, :], start=True, stop=True))
                if eng is DVE:
                    wait(DVE, "ps_st", b, c + 1)
                    wait(DVE, "ps_inter", b.prev())
                    if c == 0:
                        sig("state", DVE.tensor_copy(S[:, 0, :], bank_of("st0")[0:NS, :]))
                    else:
                        wait(DVE, "state", b, c)
                        sig("st_tmp", DVE.tensor_tensor(
                            S[:, c, :].rearrange("p (h n) -> p h n", h=H),
                            S[:, c - 1, :].rearrange("p (h n) -> p h n", h=H),
                            total[:, c * H:(c + 1) * H].unsqueeze(2).to_broadcast([NS, H, HD]), ALU.mult))
                        wait(DVE, "st_tmp", b, c)
                        sig("state", DVE.tensor_tensor(S[:, c, :], S[:, c, :], bank_of(f"st{c}")[0:NS, :], ALU.add))

        def mix_mask(eng, b, u):
            if eng is PO:
                HF = NC // 2
                q, f = divmod(u, 2)
                wait(PO, "a_split", b)
                wait(PO, "ps_seg", b if u else b.prev(), u if u else None)
                shape = [P, HF, 2, P]
                up = upper[:, :].unsqueeze(1).unsqueeze(1).to_broadcast(shape)
                for dst, src in ((Ua_hi, a_hi), (Ua_lo, a_lo)):
                    last = PO.tensor_tensor(dst[:, :].rearrange("p (c j t) -> p c j t", c=HF, j=2), up,
                                            src[:, f * HF:(f + 1) * HF, 2 * q:2 * q + 2].bitcast(F32).unsqueeze(3).to_broadcast(shape),
                                            ALU.mult)
                sig("Ua", last)

        def mix_decay(eng, b, q, f):
            HF = NC // 2
            cs = slice(f * HF, (f + 1) * HF)
            u = 2 * q + f
            half = slice(f * T, (f + 1) * T)
            if eng is PE:
                wait(PE, "Ua", b, u + 1)
                ps = mix_bank(b, f"seg{u}")
                PE.matmul(ps[:, :], strict_r[:, :], Ua_hi[:, :], start=True, stop=False)
                sig("ps_seg", PE.matmul(ps[:, :], strict_r[:, :], Ua_lo[:, :], start=False, stop=True))
            if eng is AC:
                wait(AC, "ps_seg", b, u + 1)
                wait(AC, "ps_st", b)
                if q >= 2:
                    wait(AC, "ps_intra", b, q - 1)
                sig("segexp", AC.activation(Wt[:, q % 2, half], bank_of(f"seg{u}")[:, :], ACT.Exp))
            if eng is DVE:
                wait(DVE, "segexp", b, u + 1)
                wv = Wt[:, q % 2, half].rearrange("p (c j t) -> p c j t", c=HF, j=2)
                sig("W", DVE.tensor_tensor(wv, wv, Gm[:, cs, :].unsqueeze(2).to_broadcast([P, HF, 2, P]), ALU.mult))
            if u + 1 < 2 * NQ:
                mix_mask(eng, b, u + 1)

        def mix_pair(eng, b, q):
            R = slice(DTROW, DTROW + H)
            cols = (NC - 1) * P
            if eng is PE:
                wait(PE, "cum_lo", b)
                ps = mix_bank(b, f"decb{q}")
                sel = pairs[R, q * P:(q + 1) * P]
                PE.matmul(ps[:, 0:cols], sel, rows_hi[R, 0:cols], start=True, stop=False)
                sig("ps_decb", PE.matmul(ps[:, 0:cols], sel, rows_lo[R, 0:cols], start=False, stop=True))
                wait(PE, "state", b)
                ps = mix_bank(b, f"inter{q}")
                for c in range(1, NC):
                    last = PE.matmul(ps[:, tok(c)], S[:, c - 1, q * P:(q + 1) * P], CT[:, tok(c)], start=True, stop=True)
                sig("ps_inter", last)
                ps = mix_bank(b, f"XT{q}")
                w = slice(q * P, (q + 1) * P)
                sig("ps_XT", mm3(ps[:, :], [(wx_hi[:, w], wx_lo[:, w], xT_hi[:, :], xT_lo[:, :])]))
                wait(PE, "W", b, 2 * q + 2)
                ps = mix_bank(b, f"intra{q}")
                for c in range(NC):
                    for j in range(2):
                        h = 2 * q + j
                        at = (c * 2 + j) * P
                        last = PE.matmul(ps[j * HD:(j + 1) * HD, tok(c)], Xd[:, c, h * HD:(h + 1) * HD],
                                         Wt[:, q % 2, at:at + P], start=True, stop=True)
                sig("ps_intra", last)
            if eng is AC:
                wait(AC, "ps_decb", b, q + 1)
                wait(AC, "skip", b if q else b.prev(), q if q else None)
                sig("decb", AC.copy(decb[:, P:T], bank_of(f"decb{q}")[:, 0:cols]))
            if eng is DVE:
                wait(DVE, "ps_inter", b, q + 1)
                wait(DVE, "decb", b, q + 1)
                sig("inter", DVE.tensor_tensor(decb[:, P:T], bank_of(f"inter{q}")[:, P:T], decb[:, P:T], ALU.mult))
                wait(DVE, "ps_XT", b, q + 1)
                wait(DVE, "inter", b, q + 1)
                wait(DVE, "gated", b if q else b.prev(), q if q else None)
                sig("skip", DVE.scalar_tensor_tensor(yt[:, :], bank_of(f"XT{q}")[:, :], d_col[:, q:q + 1], decb[:, :],
                                                     ALU.mult, ALU.add))
                wait(DVE, "ps_intra", b, q + 1)
                wait(DVE, "skip", b, q + 1)
                sig("y", DVE.tensor_tensor(yt[:, :], bank_of(f"intra{q}")[:, :], yt[:, :], ALU.add))
                wait(DVE, "y", b, q + 1)
                wait(DVE, "zg", b, q + 1)
                sig("gated", DVE.tensor_tensor(zg[:, q, :], yt[:, :], zg[:, q, :], ALU.mult))

        def mix_out(eng, b):
            if eng is PE:
                wait(PE, "gated", b)
                ps = mix_bank(b, "out")
                for c in range(NC):
                    for q in range(NQ):
                        last = PE.matmul(ps[:, tok(c)], zg[:, q, tok(c)], wout[:, q, :], start=(q == 0), stop=(q == NQ - 1))
                sig("ps_out", last)
            if eng is DVE:
                wait(DVE, "ps_out", b)
                sig("v", DVE.tensor_tensor(x_in[:, :, :], bank_of("out")[:, :].rearrange("p (c d) -> p c d", c=NC),
                                           x_in[:, :, :], ALU.add))

        def layer_norm(eng, b, pre, src, dst, done, before_write):
            veps, lnv, r0, t0, t1, rstd = (nrm[:, k, :] for k in range(6))
            if eng is DVE:
                n = [0]
                for c in range(NC):
                    last = DVE.bn_stats(st6[:, c, :], src[:, c, :])
                link(DVE, pre + "_v", b, last, n)
                alone(DVE)
                for c in range(NC):
                    last = DVE.bn_aggr(mv[:, c, :], st6[:, c, :])
                link(DVE, pre + "_v", b, last, n)
                link(DVE, pre + "_v", b, DVE.tensor_scalar(veps, mv[:, :, 1], LN_EPS, None, ALU.add), n)
                wait(DVE, pre + "_s", b)
                link(DVE, pre + "_v", b, DVE.tensor_tensor(t0, r0, r0, ALU.mult), n)
                link(DVE, pre + "_v", b, DVE.tensor_tensor(t1, t0, veps, ALU.mult), n)
                link(DVE, pre + "_v", b, DVE.tensor_scalar(t0, t1, -0.5, 1.5, ALU.mult, ALU.add), n)
                link(DVE, pre + "_v", b, DVE.tensor_tensor(rstd, r0, t0, ALU.mult), n)
                before_write()
                for c in range(NC):
                    last = DVE.tensor_scalar(dst[:, c, :], src[:, c, :], mv[:, c, 0:1], rstd[:, c:c + 1],
                                             ALU.subtract, ALU.mult)
                sig(done, last)
                wait(DVE, done, b)
            if eng is AC:
                wait(AC, pre + "_v", b, 3)
                sig(pre + "_s", AC.activation(lnv, veps, ACT.Ln))
                wait(AC, pre + "_s", b, 1)
                sig(pre + "_s", AC.activation(r0, lnv, ACT.Exp, scale=-0.5))

        def route_norm(eng, b):
            if eng is DVE:
                wait(DVE, "v", b)
            layer_norm(eng, b, "ln1", x_in, x1, "x1", lambda: wait(DVE, "acc", b.prev()))

        def route_transpose(eng, b):
            if eng is PE:
                wait(PE, "x1", b)
                wait(PE, "acc", b.prev())
                for c in range(NC):
                    last = PE.transpose(rb[:, tok(c)], x1[:, c, :], ident[:, :])
                sig("ps_x1T", last)
            if eng is AC:
                wait(AC, "ps_x1T", b)
                wait(AC, "xw", b.prev())
                sig("x1T", AC.copy(x1T, rb[:, :]))

        def route_logits(eng, b):
            if eng is PE:
                wait(PE, "x1T", b)
                for c in range(NC):
                    last = PE.matmul(rb[:, tok(c)], x1T[:, tok(c)], router[:, :], start=True, stop=True)
                sig("ps_lg", last)
            if eng is AC:
                wait(AC, "ps_lg", b)
                wait(AC, "gelu_hi", b.prev())
                wait(AC, "gelu_lo", b.prev())
                sig("lg", AC.copy(lg[:, :, :].rearrange("p (c r) e -> p c (r e)", c=NC),
                                  rb[:, :].rearrange("p (c n) -> p c n", c=NC)[:, :, 0:NR * E]))

        def route_weights(eng, b):
            NGR = NC * NR
            wide3 = [P, NGR, E]
            if eng is DVE:
                n = [0]
                wait(DVE, "lg", b)
                wait(DVE, "gelu_lo", b.prev())
                alone(DVE)
                for g in range(NGR):
                    last = DVE.max(mx[:, g, :], lg[:, g, :])
                link(DVE, "rt_v", b, last, n)
                alone(DVE)
                for g in range(NGR):
                    last = DVE.max_index(ix[:, g, :], mx[:, g, :], lg[:, g, :])
                link(DVE, "rt_v", b, last, n)
                link(DVE, "rt_v", b, DVE.tensor_tensor(lg[:, :, :], lg[:, :, :], mx[:, :, 0:1].to_broadcast(wide3),
                                                       ALU.subtract), n)
                for k in range(TOPK):
                    last = DVE.tensor_tensor(hot[:, k, :, :], iota_e[:, :].unsqueeze(1).to_broadcast(wide3),
                                             ix[:, :, k:k + 1].to_broadcast(wide3), ALU.is_equal)
                link(DVE, "rt_v", b, last, n)
                link(DVE, "rt_v", b, DVE.tensor_tensor(hot[:, 0], hot[:, 0], hot[:, 1], ALU.add), n)
                link(DVE, "rt_v", b, DVE.tensor_tensor(hot[:, 0], hot[:, 0], hot[:, 2], ALU.add), n)
                wait(DVE, "rt_s", b)
                link(DVE, "rt_v", b, DVE.tensor_tensor(lg[:, :, :], lg[:, :, :], hot[:, 0], ALU.mult), n)
                link(DVE, "rt_v", b, DVE.tensor_reduce(ssum[:, :], lg[:, :, :], AX.X, ALU.add), n)
                wait(DVE, "ps_dwT", b.prev())
                sig("dw", DVE.reciprocal(srec[:, :], ssum[:, :]))
                wait(DVE, "dw", b)
                lv = lg[:, :, :].rearrange("p (c r) e -> p c r e", c=NC)
                rv = srec[:, :].rearrange("p (c r) -> p c r", c=NC)
                for r, dst in ((0, dwpad[:, :, 0:E]), (1, dw2_new[:, :, :]), (2, dwpad[:, :, B2ROW:B2ROW + E])):
                    last = DVE.tensor_tensor(dst, lv[:, :, r, :], rv[:, :, r:r + 1].to_broadcast([P, NC, E]), ALU.mult)
                sig("dwr", last)
            if eng is AC:
                wait(AC, "rt_v", b, 3)
                sig("rt_s", AC.activation(lg[:, :, :], lg[:, :, :], ACT.Exp))

        def route_rows(eng, b):
            R1 = slice(0, E)
            if eng is PE:
                wait(PE, "lg", b)
                wait(PE, "dwr", b)
                alone(PE)
                for c in range(NC):
                    last = PE.transpose(rb[0:DTROW, tok(c)], dwpad[:, c, :], ident[:, :])
                sig("ps_dwT", last)
            if eng is AC:
                wait(AC, "ps_dwT", b)
                wait(AC, "ps_b2", b.prev())
                sig("dwT", AC.copy(rows[0:DTROW, :], rb[0:DTROW, :]))
            if eng is DVE:
                wait(DVE, "dwT", b)
                wait(DVE, "ps_row", b.prev())
                sig("dw_hi", DVE.tensor_copy(rows_hi[R1, :], rows[R1, :]))
                wait(DVE, "dw_hi", b)
                sig("dw_lo", DVE.tensor_tensor(rows_lo[R1, :], rows[R1, :], rows_hi[R1, :].bitcast(F32), ALU.subtract))

        def expert_prep(eng, b, e):
            at = (e + 2) % NH
            if eng is PE:
                wait(PE, "dw_lo", b)
                if e == 0:
                    wait(PE, "dwT", b)
                else:
                    wait(PE, "xw", b, e)
                sel = pick[0:E, e:e + 1].to_broadcast([E, P])
                PE.matmul(rb[:, :], sel, rows_hi[0:E, :], start=True, stop=False)
                sig("ps_row", PE.matmul(rb[:, :], sel, rows_lo[0:E, :], start=False, stop=True))
            if eng is DVE:
                wait(DVE, "ps_row", b, e + 1)
                if e >= 2:
                    wait(DVE, "xw_hi", b, e - 1)
                    wait(DVE, "xw_lo", b, e - 1)
                sig("xw", DVE.tensor_tensor(wide[e % 2], rb[:, :], x1T, ALU.mult))
            if eng is AC:
                wait(AC, "xw", b, e + 1)
                wait(AC, "ps_y", b.prev())
                if e >= 4:
                    wait(AC, "ps_h", b, e - 3)
                elif e >= 2 and (b.reg is not None or b.off < NB - 1):
                    wait(AC, "ps_zg", Batch(b.reg, b.off + 1))
                sig("xw_hi", AC.copy(sp_hi[:, at, :], wide[e % 2]))
            if eng is PO:
                wait(PO, "xw_hi", b, e + 1)
                sig("xw_lo", PO.tensor_tensor(sp_lo[:, at, :], wide[e % 2], sp_hi[:, at, :].bitcast(F32), ALU.subtract))

        def expert_in(eng, b, e):
            if eng is PE:
                at = (e + 2) % NH
                if e == 0:
                    wait(PE, "comb", b.prev())
                wait(PE, "xw_lo", b, e + 1)
                for hc in range(NH):
                    w = slice(hc * P, (hc + 1) * P)
                    last = mm3(hb[hc][:, :], [(w1_hi[:, e, w], w1_lo[:, e, w], sp_hi[:, at, :], sp_lo[:, at, :])],
                               start=(e == 0), stop=(e == E - 1))
                sig("ps_h", last)

        def expert_gelu(eng, b):
            for k in range(NH):
                g = wide[k % 2]
                if eng is AC:
                    wait(AC, "ps_h", b)
                    if k >= 2:
                        wait(AC, "gelu_hi", b, k - 1)
                        wait(AC, "gelu_lo", b, k - 1)
                    else:
                        wait(AC, "xw_hi", b)
                        wait(AC, "xw_lo", b)
                    sig("gelu", AC.activation(g, hb[k][:, :], ACT.Gelu))
                if eng is DVE:
                    wait(DVE, "ps_h", b)
                    wait(DVE, "gelu", b, k + 1)
                    sig("gelu_hi", DVE.tensor_copy(sp_hi[:, k, :], g))
                if eng is PO:
                    wait(PO, "gelu_hi", b, k + 1)
                    sig("gelu_lo", PO.tensor_tensor(sp_lo[:, k, :], g, sp_hi[:, k, :].bitcast(F32), ALU.subtract))

        def expert_b2(eng, b):
            R = slice(B2ROW, B2ROW + E)
            if eng is PE:
                wait(PE, "xw", b)
                for c in range(NC):
                    last = PE.matmul(rb[:, tok(c)], rows[R, tok(c)], b2_sb[R, :], start=True, stop=True)
                sig("ps_b2", last)
            if eng is DVE:
                wait(DVE, "ps_b2", b)
                wait(DVE, "stored", b.prev())
                DVE.tensor_copy(dw2[:, :, :], dw2_new[:, :, :])
                sig("acc", DVE.tensor_tensor(acc[:, :, :], rb[:, :].rearrange("p (c d) -> p c d", c=NC), x1, ALU.add))
                wait(DVE, "acc", b)

        def expert_out(eng, b, c):
            per = E + 1
            for g in range(NG):
                m = c * NG + g
                if eng is PE:
                    if m == 0:
                        wait(PE, "gelu_lo", b)
                    if m < NH:
                        wait(PE, "gelu", b, m + 1)
                    else:
                        before = m - NH
                        wait(PE, "comb", b, before // NG * per + (before % NG + 1) * EG)
                    w = slice(g * T, (g + 1) * T)
                    sig("ps_y", mm3(hb[m % NH][:, :], [(sp_hi[:, k, tok(c)], sp_lo[:, k, tok(c)], w2_hi[:, k, w], w2_lo[:, k, w])
                                                       for k in range(NH)]))
                if eng is DVE:
                    wait(DVE, "ps_y", b, m + 1)
                    for s in range(EG):
                        e = g * EG + s
                        n = c * per + e
                        ps, w, dst = hb[m % NH][:, s * D:(s + 1) * D], dw2[:, c, e:e + 1], (acc[:, c, :], acc_odd[:, :])[e % 2]
                        if e >= 2:
                            wait(DVE, "comb", b, n - 1)
                        if e == 1:
                            sig("comb", DVE.tensor_scalar(dst, ps, w, None, ALU.mult))
                        else:
                            sig("comb", DVE.scalar_tensor_tensor(dst, ps, w, dst, ALU.mult, ALU.add))
            if eng is DVE:
                wait(DVE, "comb", b, (c + 1) * per - 1)
                sig("comb", DVE.tensor_tensor(acc[:, c, :], acc[:, c, :], acc_odd[:, :], ALU.add))
                wait(DVE, "comb", b, (c + 1) * per)

        def expert_norm(eng, b):
            if eng is DVE:
                wait(DVE, "comb", b)
            layer_norm(eng, b, "ln2", acc, acc, "o", lambda: None)
            store(eng, b)

        def store(eng, b):
            if eng is SP:
                wait(SP, "o", b)
                sig("stored", SP.dma_start(out_rows(b), acc[:, :, :]))

        def experts(eng, b, es, ahead):
            for e in es:
                while ahead[0] <= min(e + 2, E - 1):
                    expert_prep(eng, b, ahead[0])
                    ahead[0] += 1
                expert_in(eng, b, e)

        def body(eng, b, front_next, norm_before=True):
            p, nxt = b.prev(), Batch(b.reg, b.off + 1)
            ahead = [2]
            mix_silu_split(eng, b)
            expert_prep(eng, p, 0)
            mix_X(eng, b)
            expert_prep(eng, p, 1)
            if norm_before:
                expert_norm(eng, p.prev())
            expert_in(eng, p, 0)
            mix_zg(eng, b)
            experts(eng, p, [1], ahead)
            mix_scores(eng, b)
            mix_mask(eng, b, 0)
            experts(eng, p, [2], ahead)
            mix_states(eng, b)
            e = 3
            for q in range(NQ):
                for f in range(2):
                    mix_decay(eng, b, q, f)
                    experts(eng, p, [e], ahead)
                    e += 1
                mix_pair(eng, b, q)
            experts(eng, p, range(e, E), ahead)
            expert_gelu(eng, p)
            expert_b2(eng, p)
            mix_out(eng, b)
            route_norm(eng, b)
            expert_out(eng, p, 0)
            if front_next:
                mix_load_next(eng, b)
            route_transpose(eng, b)
            expert_out(eng, p, 1)
            route_logits(eng, b)
            if front_next:
                mix_x(eng, nxt)
            route_weights(eng, b)
            expert_out(eng, p, 2)
            if front_next:
                mix_dt(eng, nxt)
                mix_bc(eng, nxt)
            route_rows(eng, b)
            if front_next:
                mix_z(eng, nxt)
            expert_out(eng, p, 3)

        def mixer_alone(eng, b):
            mix_x(eng, b)
            mix_dt(eng, b)
            mix_bc(eng, b)
            mix_z(eng, b)
            mix_silu_split(eng, b)
            mix_X(eng, b)
            split_expert_weights(eng, range(0, 4))
            mix_zg(eng, b)
            split_expert_weights(eng, range(4, 8))
            mix_scores(eng, b)
            mix_mask(eng, b, 0)
            mix_states(eng, b)
            for q in range(NQ):
                mix_decay(eng, b, q, 0)
                mix_decay(eng, b, q, 1)
                split_expert_weights(eng, range(8 + 4 * q, 12 + 4 * q))
                mix_pair(eng, b, q)
            mix_out(eng, b)
            expert_weights_ready(eng)
            route_norm(eng, b)
            mix_load_next(eng, b)
            route_transpose(eng, b)
            route_logits(eng, b)
            nxt = Batch(None, 1)
            mix_x(eng, nxt)
            route_weights(eng, b)
            mix_dt(eng, nxt)
            mix_bc(eng, nxt)
            route_rows(eng, b)
            mix_z(eng, nxt)

        def mixture_alone(eng, b):
            ahead = [0]
            experts(eng, b, [0], ahead)
            expert_norm(eng, b.prev())
            experts(eng, b, range(1, E), ahead)
            expert_gelu(eng, b)
            expert_b2(eng, b)
            for c in range(NC):
                expert_out(eng, b, c)
            expert_norm(eng, b)

        def program(eng):
            waited[id(eng)] = {}
            setup(eng)
            mixer_alone(eng, Batch(None, 0))
            body(eng, Batch(None, 1), True, norm_before=False)
            waited[id(eng)] = {}
            with eng.Fori(2, NB - 1) as i:
                body(eng, Batch(i, 0), True)
            waited[id(eng)] = {}
            body(eng, Batch(None, NB - 1), False)
            mixture_alone(eng, Batch(None, NB - 1))
            if eng is SP:
                wait(SP, "stored", Batch(None, NB - 1))

        product("dwr", 1)
        block = ctx.enter_context(nc.Block())

        @block.sync
        def _(eng):
            program(SP)

        @block.tensor
        def _(eng):
            program(PE)

        @block.vector
        def _(eng):
            program(DVE)

        @block.scalar
        def _(eng):
            program(AC)

        @block.gpsimd
        def _(eng):
            program(PO)

        for p in prods.values():
            written = 3 if p.name != "x_in" else 2
            assert p.done % p.n == 0 and p.done // p.n >= written, (p.name, p.done, p.n)


def kernel(L0_attn_x, L0_attn_Wz, L0_attn_Win, L0_attn_Wzg, L0_attn_Wout, L0_attn_dt_bias, L0_attn_A_log,
           L0_attn_D_param, L0_ffn_P_w, L0_ffn_U1, L0_ffn_U2, L0_ffn_U3, L0_ffn_W1, L0_ffn_W2, L0_ffn_b2):
    import concourse.bacc as bacc
    from concourse.bass_utils import run_bass_kernel_spmd

    lay = np.ascontiguousarray
    w2 = np.asarray(L0_ffn_W2)
    arrays = dict(
        x=lay(L0_attn_x), Wz=lay(L0_attn_Wz), Win=lay(L0_attn_Win), Wzg=lay(L0_attn_Wzg), Wout=lay(L0_attn_Wout),
        dt_bias=lay(L0_attn_dt_bias), A_log=lay(L0_attn_A_log), D_param=lay(L0_attn_D_param), P_w=lay(L0_ffn_P_w),
        U1T=lay(np.asarray(L0_ffn_U1).T), U2T=lay(np.asarray(L0_ffn_U2).T), U3T=lay(np.asarray(L0_ffn_U3).T),
        W1T=lay(np.asarray(L0_ffn_W1).transpose(2, 0, 1)),
        W2T=lay(w2.transpose(2, 0, 1).reshape(w2.shape[2], -1)),
        b2=lay(L0_ffn_b2),
    )
    nc = bacc.Bacc("TRN2", target_bir_lowering=False, num_devices=1)
    aps = [nc.dram_tensor("in_" + k, v.shape, mybir.dt.from_np(v.dtype), kind="ExternalInput").ap() for k, v in arrays.items()]
    res = nc.dram_tensor("result", (NB, T, D), F32, kind="ExternalOutput").ap()
    layer_program(nc, *aps, res)
    r = run_bass_kernel_spmd(nc, [{"in_" + k: v for k, v in arrays.items()}], core_ids=[0])
    return r.results[0]["result"]
```

```python
from contextlib import ExitStack

import numpy as np

import concourse.bass as bass
from concourse import mybir

F32 = mybir.dt.float32
F32R = mybir.dt.float32r
I32 = mybir.dt.int32
U32 = mybir.dt.uint32
ALU = mybir.AluOpType
ACT = mybir.ActivationFunctionType
AX = mybir.AxisListType

P = 128
D = 128
NB, T = 16, 512
NC = T // P
H, HD, NS = 8, 64, 64
NQ = H // 2
DI = H * HD
DZ = 2 * D
NK = DZ // P
E, TOPK = 12, 3
HID = 512
NH = HID // P
NG = E * D // T
EG = E // NG
NR = 3
B2ROW = 32
DTROW = 64
LOROW = 32
LN_EPS = 1e-5

MIX_USES = (
    [("xT", "xT", 1), ("dtB", "dt_raw", 1), ("BC", "BC", 1)]
    + [(f"z{k}", "silu", k + 1) for k in range(NK)]
    + [(f"X{c}", "Xd", c + 1) for c in range(NC)]
    + [(f"zg{q}", "zg", q + 1) for q in range(NQ)]
    + [("cum", "cumexp", 1), ("ends", "ends", 1), ("G", "Gm", 1)]
    + [("st01", "state", 2), ("st2", "state", 3)]
    + [("seg0", "segexp", 1)]
    + [u for q in range(NQ) for u in (
        (f"decb{q}", "decb", q + 1), (f"inter{q}", "inter", q + 1), (f"XT{q}", "skip", q + 1),
        (f"seg{2 * q + 1}", "segexp", 2 * q + 2), (f"seg{2 * q + 2}", "segexp", 2 * q + 3), (f"intra{q}", "y", q + 1))
       if u[0] != f"seg{2 * NQ}"]
    + [("out", "v", 1)]
)
MIX_USE = {u[0]: n for n, u in enumerate(MIX_USES)}
NX = 3


class Batch:

    def __init__(self, reg, off):
        self.reg, self.off = reg, off

    def prev(self):
        return Batch(self.reg, self.off - 1)

    def index(self):
        if self.reg is None:
            return self.off
        return self.reg + self.off if self.off else self.reg


class Product:

    def __init__(self, sem, name, n, step=1):
        self.sem, self.name, self.n, self.step = sem, name, n, step
        self.done = 0


def layer_program(nc, x, Wz, Win, Wzg, Wout, dt_bias, A_log, D_param, P_w, U1T, U2T, U3T, W1T, W2T, b2, out):
    ctx = ExitStack()
    with ctx:
        def sb(name, shape, dt=F32):
            return ctx.enter_context(nc.sbuf_tensor(name, shape, dt))

        w1_hi, w1_lo = sb("w1_hi", [P, E, HID], F32R), sb("w1_lo", [P, E, HID], F32R)
        w2_hi, w2_lo = sb("w2_hi", [P, NH, E * D], F32R), sb("w2_lo", [P, NH, E * D], F32R)
        wbc_hi, wbc_lo = sb("wbc_hi", [P, 2 * NS], F32R), sb("wbc_lo", [P, 2 * NS], F32R)
        wz_hi, wz_lo = sb("wz_hi", [P, DZ], F32R), sb("wz_lo", [P, DZ], F32R)
        wx_hi, wx_lo = sb("wx_hi", [P, DI], F32R), sb("wx_lo", [P, DI], F32R)
        wzg_hi, wzg_lo = sb("wzg_hi", [P, NK, DI], F32R), sb("wzg_lo", [P, NK, DI], F32R)
        wbdt = sb("wbdt", [P, P])
        wout = sb("wout", [P, NQ, D])
        router = sb("router", [P, P])
        b2_sb = sb("b2_sb", [NS, D])
        ident, upper = sb("ident", [P, P]), sb("upper", [P, P])
        strict_r = sb("strict_r", [P, P], F32R)
        pick_f, pick = sb("pick_f", [P, E]), sb("pick", [P, E], F32R)
        pairs = sb("pairs", [P, DI], F32R)
        iota_i, iota_e = sb("iota_i", [P, E], I32), sb("iota_e", [P, E])
        bias_b, neg_a, d_col = sb("bias_b", [P, H]), sb("neg_a", [P, H]), sb("d_col", [P, NQ])
        x_in = sb("x_in", [P, NC, D])
        xT = sb("xT", [P, T])
        xT_hi, xT_lo = sb("xT_hi", [P, T], F32R), sb("xT_lo", [P, T], F32R)
        BT, CT = sb("BT", [NS, T]), sb("CT", [NS, T])
        B_tok = sb("B_tok", [P, NC, NS])
        Xd = sb("Xd", [P, NC, DI])
        Ua_hi, Ua_lo = sb("Ua_hi", [P, T], F32R), sb("Ua_lo", [P, T], F32R)
        Gm = sb("Gm", [P, NC, P])
        Wt = sb("Wt", [P, 2, 2 * T])
        S = sb("S", [P, NC - 1, DI])
        pw, ut = S[0:P_w.shape[0], 0, 0:D], S[0:P_w.shape[0], 0, D:2 * D]
        decb = sb("decb", [P, T])
        yt = sb("yt", [P, T])
        zg = sb("zg", [P, NQ, T])
        dt_s = sb("dt_s", [P, 6, NC * H])
        delta, a = sb("delta", [P, NC, H]), sb("a", [P, NC, H])
        a_hi, a_lo = sb("a_hi", [P, NC, H], F32R), sb("a_lo", [P, NC, H], F32R)
        ends = sb("ends", [P, (NC - 1) * H])
        total = sb("total", [NS, NC * H])
        silu = Wt[:, 0, :].rearrange("p (k t) -> p k t", k=NK)
        pairs_f = Wt[:, 1, 0:DI]
        strict = Wt[:, 0, 0:P]
        Xde = Wt[:, :, :].rearrange("p a b -> p (a b)")[:, 0:(NC - 1) * DI].rearrange("p (c n) -> p c n", c=NC - 1)
        rows = sb("rows", [P, T])
        rows_s = sb("rows_s", [P, T], F32R)
        fbuf = sb("fbuf", [P, 4, T])
        x1 = fbuf[:, 0, :].rearrange("p (c d) -> p c d", c=NC)
        x1T = fbuf[:, 1, :]
        acc = sb("acc", [P, NC, D])
        acc_odd = sb("acc_odd", [P, D])
        wide = [fbuf[:, 2, :], fbuf[:, 3, :]]
        sp_hi, sp_lo = sb("sp_hi", [P, NH, T], F32R), sb("sp_lo", [P, NH, T], F32R)
        lg = fbuf[:, 3, 0:NC * NR * E].rearrange("p (g e) -> p g e", e=E)
        mx = fbuf[:, 3, NC * NR * E:NC * NR * (E + 8)].rearrange("p (g e) -> p g e", e=8)
        ix = sb("ix", [P, NC * NR, 8], U32)
        hot = fbuf[:, 2, 0:TOPK * NC * NR * E].rearrange("p (k g e) -> p k g e", k=TOPK, g=NC * NR)
        ssum, srec = sb("ssum", [P, NC * NR]), sb("srec", [P, NC * NR])
        dw2_new, dw2 = sb("dw2_new", [P, NC, E]), sb("dw2", [P, NC, E])
        dwpad = sb("dwpad", [P, NC, DTROW])
        st6, mv, nrm = sb("st6", [P, NC, 6]), sb("mv", [P, NC, 2]), sb("nrm", [P, 6, NC])

        xb = [ctx.enter_context(nc.psum_tensor(f"mix_bank{n}", [P, T], F32)) for n in range(NX)]
        hb = [ctx.enter_context(nc.psum_tensor(f"exp_bank{n}", [P, T], F32)) for n in range(NH)]
        rb = ctx.enter_context(nc.psum_tensor("row_bank", [P, T], F32))

        prods = {}

        def product(name, n, step=1):
            prods[name] = Product(ctx.enter_context(nc.semaphore(name)), name, n, step)

        for name, n in dict(
            ps_xT=1, xT=1, xT_lo=1, ps_dtB=1, dt_raw=1, dt_v=15, dt_s=2, dt_q=1, a_split=1, ps_BC=1, BC=1,
            ps_z=NK, tanh=NK, silu=NK, silu_hi=NK, silu_lo=NK, ps_X=NC, Xd=NC, ps_zg=NQ, zg=NQ,
            ps_G=1, Gm=1, ps_cum=1, cumexp=1, cum_hi=1, cum_lo=1, ps_ends=1, ends=1, Xde=NC - 1,
            ps_st=2, state=NC - 1, st_tmp=NC - 2, ps_decb=NQ, decb=NQ, Ua=2 * NQ, Ua_lo=2 * NQ, ps_seg=2 * NQ, segexp=2 * NQ,
            W=2 * NQ, ps_inter=NQ, inter=NQ, ps_XT=NQ, skip=NQ, ps_intra=NQ, y=NQ, gated=NQ, ps_out=1, v=1,
            ln1_v=7, ln1_s=2, x1=1, ps_x1T=1, x1T=1, ps_lg=1, lg=1, rt_v=8, rt_s=1, dw=1, ps_dwT=1, dwT=1, dw_hi=1,
            dw_lo=1, ps_row=E, xw=E, xw_hi=E, xw_lo=E, ps_h=E - 1, ps_h_full=NH, gelu=NH,
            gelu_hi=NH, gelu_lo=NH // 2, gelu_lo_v=NH // 2, ps_b2=1, acc=1,
            ps_y=NC * NG, comb=NC * (E + 1), ln2_v=7, ln2_s=2, o=1,
        ).items():
            product(name, n)
        product("x_in", 1, 16)
        product("stored", 1, 16)
        sems = {n: ctx.enter_context(nc.semaphore("set_" + n)) for n in
                ("mix_w", "win", "wbdt", "small", "decay_par", "ring0", "ring1", "ring2", "ring3",
                 "w_hi", "w_lo0", "w_lo1", "masks", "cast", "chain", "alog", "ps_r", "router", "pad")}

        waited = {}

        def wait(eng, name, b, k=None):
            p = prods[name]
            v = b.off * p.n * p.step + (p.n if k is None else k) * p.step
            seen = waited.setdefault(id(eng), {})
            if (b.reg is None and v <= 0) or seen.get(name, -10**9) >= v:
                return
            seen[name] = v
            eng.wait_ge(p.sem, v if b.reg is None else b.reg * (p.n * p.step) + v)

        def alone(eng):
            eng.nop(nofuse=True)

        def sig(name, ins):
            p = prods[name]
            p.done += 1
            ins.then_inc(p.sem, p.step)

        def link(eng, name, b, ins, count):
            count[0] += 1
            sig(name, ins)
            wait(eng, name, b, count[0])

        def mm3(ps, pairs, start=True, stop=True, before=lambda j: None):
            last = None
            n = len(pairs)
            for j, (s_hi, s_lo, m_hi, m_lo) in enumerate(pairs):
                before(j)
                nc.tensor.matmul(ps, s_hi, m_hi, start=start and j == 0, stop=False)
                nc.tensor.matmul(ps, s_hi, m_lo, start=False, stop=False)
                last = nc.tensor.matmul(ps, s_lo, m_hi, start=False, stop=stop and j == n - 1)
            return last

        def mix_bank(b, use):
            n = MIX_USE[use]
            if n >= NX:
                before, owner = n - NX, b
            else:
                before, owner = max(m for m in range(len(MIX_USES)) if m % NX == n), b.prev()
            _, reader, k = MIX_USES[before]
            wait(nc.tensor, reader, owner, k)
            return xb[n % NX]

        def bank_of(use):
            return xb[MIX_USE[use] % NX]

        tok = lambda c: slice(c * P, (c + 1) * P)
        PE, DVE, AC, PO, SP = nc.tensor, nc.vector, nc.scalar, nc.gpsimd, nc.sync

        NW = 2 * E
        RING = 4
        mix_stage = Xd[:, :, :].rearrange("p c n -> p (c n)")
        st_win, st_wz = mix_stage[:, 0:648], mix_stage[:, 648:904]
        st_wzg = mix_stage[:, 904:904 + NK * DI].rearrange("p (k n) -> p k n", k=NK)

        def w_tile(k):
            if k < E:
                return W1T[:, k, :], w1_hi[:, k, :], w1_lo[:, k, :]
            kc, g = divmod(k - E, NG)
            cols = slice(g * T, (g + 1) * T)
            return W2T[kc * P:(kc + 1) * P, cols], w2_hi[:, kc, cols], w2_lo[:, kc, cols]

        def setup(eng):
            if eng is SP:
                SP.dma_start(x_in[:, :, :], x[0].rearrange("(c p) d -> p c d", p=P)).then_inc(prods["x_in"].sem, 16)
                SP.dma_start(st_win, Win[:, :]).then_inc(sems["win"], 16)
                SP.dma_start(st_wz, Wz[:, :]).then_inc(sems["mix_w"], 16)
                SP.dma_start(st_wzg, Wzg.rearrange("(k p) n -> p k n", p=P)).then_inc(sems["mix_w"], 16)
                SP.dma_start(bias_b[:, :], dt_bias.partition_broadcast(P)).then_inc(sems["decay_par"], 16)
                SP.dma_start(neg_a[:, :], A_log.partition_broadcast(P)).then_inc(sems["decay_par"], 16)
                for k in range(NW):
                    if k == RING:
                        for j in range(2):
                            SP.dma_start(d_col[j * HD:(j + 1) * HD, :],
                                         D_param.rearrange("(q j) -> j q", j=2)[j, :].partition_broadcast(HD),
                                         allow_slow_non_contiguous=True).then_inc(sems["small"], 16)
                        SP.dma_start(wout[:, :, :], Wout.rearrange("(q p) n -> p q n", p=P)).then_inc(sems["small"], 16)
                        SP.dma_start(pw, P_w[:, :]).then_inc(sems["small"], 16)
                        SP.wait_ge(sems["pad"], 2)
                        for r, u in enumerate((U1T, U2T, U3T)):
                            SP.dma_start(ut[:, r * E:(r + 1) * E], u[:, :]).then_inc(sems["small"], 16)
                        SP.dma_start(b2_sb[B2ROW:B2ROW + E, :], b2[:, :]).then_inc(sems["small"], 16)
                    if k >= RING:
                        SP.wait_ge(sems["w_hi"], k - RING + 1)
                        SP.wait_ge(sems[f"w_lo{k % 2}"], (k - RING) // 2 + 1)
                        SP.wait_ge(sems[f"ring{k % RING}"], 16 * (k // RING))
                    SP.dma_start(fbuf[:, k % RING, :], w_tile(k)[0]).then_inc(sems[f"ring{k % RING}"], 16)
            if eng is PO:
                PO.memset(wbdt[:, :], 0.0).then_inc(sems["pad"], 1)
                PO.memset(ut, 0.0).then_inc(sems["pad"], 1)
                for m, v in ((ident[:, :], 0.0), (upper[:, :], 1.0), (strict, 1.0)):
                    PO.memset(m, v).then_inc(sems["masks"], 1)
                PO.memset(pick_f[:, :], 0.0).then_inc(sems["masks"], 1)
                PO.memset(pairs_f, 0.0).then_inc(sems["masks"], 1)
                PO.memset(dwpad[:, :, :], 0.0).then_inc(sems["masks"], 1)
                PO.memset(decb[:, 0:P], 0.0).then_inc(sems["masks"], 1)
                PO.iota(iota_i[:, :], pattern=[[1, E]], base=0, channel_multiplier=0).then_inc(sems["masks"], 1)
                PO.wait_ge(sems["masks"], 8)
                PO.affine_select(out=ident[:, :], in_=ident[:, :], compare_op=ALU.not_equal, fill=1.0, base=0,
                                 pattern=[[-1, P]], channel_multiplier=1).then_inc(sems["masks"], 1)
                PO.affine_select(out=upper[:, :], in_=upper[:, :], compare_op=ALU.is_ge, fill=0.0, base=0,
                                 pattern=[[1, P]], channel_multiplier=-1).then_inc(sems["masks"], 1)
                PO.affine_select(out=strict, in_=strict, compare_op=ALU.is_gt, fill=0.0, base=0,
                                 pattern=[[-1, P]], channel_multiplier=1).then_inc(sems["masks"], 1)
                PO.affine_select(out=pick_f[:, :], in_=pick_f[:, :], compare_op=ALU.not_equal, fill=1.0, base=0,
                                 pattern=[[-1, E]], channel_multiplier=1).then_inc(sems["masks"], 1)
                PO.affine_select(out=pairs_f, in_=pairs_f, compare_op=ALU.not_equal, fill=1.0, base=-DTROW,
                                 pattern=[[-1, H], [0, HD]], channel_multiplier=1).then_inc(sems["masks"], 1)
                PO.wait_ge(sems["masks"], 13)
                PO.affine_select(out=pick_f[:, :], in_=pick_f[:, :], compare_op=ALU.not_equal, fill=1.0, base=-LOROW,
                                 pattern=[[-1, E]], channel_multiplier=1).then_inc(sems["masks"], 1)
                PO.affine_select(out=pairs_f, in_=pairs_f, compare_op=ALU.not_equal, fill=1.0, base=-DTROW - LOROW,
                                 pattern=[[-1, H], [0, HD]], channel_multiplier=1).then_inc(sems["masks"], 1)
                PO.wait_ge(sems["decay_par"], 32)
                PO.wait_ge(sems["chain"], 4)
            if eng is DVE:
                DVE.wait_ge(sems["win"], 16)
                DVE.wait_ge(sems["pad"], 1)
                DVE.tensor_copy(wbdt[:, 0:NS], st_win[:, 0:NS]).then_inc(sems["wbdt"], 1)
                DVE.tensor_copy(wbdt[:, NS:NS + H], st_win[:, 2 * NS:2 * NS + H]).then_inc(sems["wbdt"], 1)
                win_parts = ((st_win[:, 0:2 * NS], wbc_hi[:, :], wbc_lo[:, :]),
                             (st_win[:, 2 * NS + H:], wx_hi[:, :], wx_lo[:, :]))
                z_parts = ((st_wz, wz_hi[:, :], wz_lo[:, :]), (st_wzg, wzg_hi[:, :, :], wzg_lo[:, :, :]))
                for n, parts in enumerate((win_parts, z_parts)):
                    if n == 1:
                        DVE.wait_ge(sems["mix_w"], 32)
                        DVE.tensor_scalar(st_wzg, st_wzg, 0.5, None, ALU.mult).then_inc(sems["chain"], 1)
                        DVE.wait_ge(sems["chain"], 2)
                    for src, hi, _ in parts:
                        last = DVE.tensor_copy(hi, src)
                    last.then_inc(sems["chain"], 1)
                    DVE.wait_ge(sems["chain"], 1 + 2 * n)
                    for src, hi, lo in parts:
                        DVE.tensor_tensor(lo, src, hi.bitcast(F32), ALU.subtract).then_inc(sems["cast"], 1)
                DVE.wait_ge(sems["masks"], 15)
                DVE.tensor_copy(strict_r[:, :], strict).then_inc(sems["cast"], 1)
                DVE.tensor_copy(pick[:, :], pick_f[:, :]).then_inc(sems["cast"], 1)
                DVE.tensor_copy(pairs[:, :], pairs_f).then_inc(sems["cast"], 1)
                DVE.tensor_copy(iota_e[:, :], iota_i[:, :]).then_inc(sems["cast"], 1)
                for c in range(NC):
                    DVE.tensor_copy(rows_s[:, tok(c)], decb[:, 0:P]).then_inc(sems["cast"], 1)
                DVE.wait_ge(sems["cast"], 8 + NC)
            if eng is PE:
                PE.wait_ge(sems["masks"], 15)

        def neg_a_ready(eng):
            if eng is AC:
                AC.wait_ge(sems["decay_par"], 32)
                AC.activation(neg_a[:, :], neg_a[:, :], ACT.Exp).then_inc(sems["alog"], 1)
            if eng is DVE:
                DVE.wait_ge(sems["alog"], 1)
                DVE.tensor_scalar(neg_a[:, :], neg_a[:, :], -1.0, None, ALU.mult).then_inc(sems["chain"], 1)

        def router_product(eng):
            if eng is PE:
                PE.wait_ge(sems["small"], 16 * 8)
                PE.wait_ge(sems["pad"], 2)
                PE.matmul(rb[:, 0:P], pw, ut, start=True, stop=True).then_inc(sems["ps_r"], 1)
            if eng is DVE:
                DVE.wait_ge(sems["ps_r"], 1)
                DVE.tensor_copy(router[:, :], rb[:, 0:P]).then_inc(sems["router"], 1)

        def split_expert_weights(eng, ks):
            for k in ks:
                _, hi, lo = w_tile(k)
                if eng is AC:
                    AC.wait_ge(sems[f"ring{k % RING}"], 16 * (k // RING + 1))
                    AC.copy(hi, fbuf[:, k % RING, :]).then_inc(sems["w_hi"], 1)
                if eng is (PO, DVE)[k % 2]:
                    eng.wait_ge(sems["w_hi"], k + 1)
                    eng.tensor_tensor(lo, fbuf[:, k % RING, :], hi.bitcast(F32), ALU.subtract).then_inc(sems[f"w_lo{k % 2}"], 1)

        def expert_weights_ready(eng):
            if eng in (PE, DVE, AC):
                eng.wait_ge(sems["w_lo0"], NW // 2)
                eng.wait_ge(sems["w_lo1"], NW // 2)
                eng.wait_ge(sems["w_hi"], NW)
            if eng is PE:
                eng.wait_ge(sems["router"], 1)

        def mix_x(eng, b):
            if eng is PE:
                wait(PE, "x_in", b)
                ps = mix_bank(b, "xT")
                for c in range(NC):
                    last = PE.transpose(ps[:, tok(c)], x_in[:, c, :], ident[:, :])
                sig("ps_xT", last)
            if eng is AC:
                wait(AC, "ps_xT", b)
                wait(AC, "ps_XT", b.prev())
                AC.copy(xT_hi[:, :], bank_of("xT")[:, :])
                sig("xT", AC.copy(xT[:, :], bank_of("xT")[:, :]))
            if eng is DVE:
                wait(DVE, "xT", b)
                wait(DVE, "ps_XT", b.prev())
                sig("xT_lo", DVE.tensor_tensor(xT_lo[:, :], xT[:, :], xT_hi[:, :].bitcast(F32), ALU.subtract))

        def mix_dt(eng, b):
            if eng is PE:
                wait(PE, "xT", b)
                ps = mix_bank(b, "dtB")
                for c in range(NC):
                    last = PE.matmul(ps[:, tok(c)], xT[:, tok(c)], wbdt[:, :], start=True, stop=True)
                sig("ps_dtB", last)
            ps = bank_of("dtB")[:, :].rearrange("p (c n) -> p c n", c=NC)
            e, u, den, one, m, q = (dt_s[:, n, :] for n in range(6))
            flat = delta[:, :, :].rearrange("p c h -> p (c h)")
            if eng is AC:
                wait(AC, "ps_dtB", b)
                wait(AC, "ps_st", b.prev())
                AC.copy(B_tok[:, :, :], ps[:, :, 0:NS])
                wait(AC, "Xd", b.prev())
                sig("dt_raw", AC.copy(delta[:, :, :], ps[:, :, NS:NS + H]))
                wait(AC, "dt_v", b, 4)
                sig("dt_s", AC.activation(e, e, ACT.Exp))
                wait(AC, "dt_v", b, 5)
                sig("dt_s", AC.activation(m, u, ACT.Ln))
            if eng is DVE:
                wait(DVE, "dt_v", b, 8)
                sig("dt_q", DVE.reciprocal(q, den))
            if eng is PO:
                n = [0]

                def step(ins):
                    link(PO, "dt_v", b, ins, n)
                    alone(PO)
                wait(PO, "dt_raw", b)
                step(PO.tensor_tensor(delta[:, :, :], delta[:, :, :], bias_b[:, :].unsqueeze(1).to_broadcast([P, NC, H]),
                                      ALU.add))
                step(PO.tensor_scalar(e, flat, 0.0, None, ALU.min))
                step(PO.tensor_scalar(flat, flat, 0.0, None, ALU.max))
                step(PO.tensor_tensor(e, e, flat, ALU.subtract))
                wait(PO, "dt_s", b, 1)
                alone(PO)
                step(PO.tensor_scalar(u, e, 1.0, None, ALU.add))
                step(PO.tensor_scalar(den, u, -1.0, None, ALU.add))
                step(PO.tensor_scalar(one, den, 0.0, None, ALU.is_equal))
                step(PO.tensor_tensor(den, den, one, ALU.add))
                wait(PO, "dt_q", b)
                step(PO.tensor_tensor(q, q, e, ALU.mult))
                wait(PO, "dt_s", b, 2)
                step(PO.tensor_tensor(q, q, m, ALU.mult))
                step(PO.tensor_tensor(one, one, e, ALU.mult))
                step(PO.tensor_tensor(q, q, one, ALU.add))
                step(PO.tensor_tensor(flat, flat, q, ALU.add))
                wait(PO, "ps_ends", b.prev())
                wait(PO, "Ua", b.prev())
                wait(PO, "Ua_lo", b.prev())
                step(PO.tensor_tensor(a[:, :, :], delta[:, :, :], neg_a[:, :].unsqueeze(1).to_broadcast([P, NC, H]), ALU.mult))
                step(PO.tensor_copy(a_hi[:, :, :], a[:, :, :]))
                sig("a_split", PO.tensor_tensor(a_lo[:, :, :], a[:, :, :], a_hi[:, :, :].bitcast(F32), ALU.subtract))

        def mix_bc(eng, b):
            if eng is PE:
                wait(PE, "xT_lo", b)
                ps = mix_bank(b, "BC")
                sig("ps_BC", mm3(ps[:, :], [(wbc_hi[:, :], wbc_lo[:, :], xT_hi[:, :], xT_lo[:, :])]))
            if eng is AC:
                wait(AC, "ps_BC", b)
                wait(AC, "ps_G", b.prev())
                wait(AC, "ps_inter", b.prev())
                AC.copy(BT[:, :], bank_of("BC")[0:NS, :])
                sig("BC", AC.copy(CT[:, :], bank_of("BC")[NS:2 * NS, :]))

        def mix_load_next(eng, b):
            if eng is SP:
                wait(SP, "ps_xT", b)
                wait(SP, "x1", b)
                sig("x_in", SP.dma_start(x_in[:, :, :], x_rows(Batch(b.reg, b.off + 1))))

        def x_rows(b):
            return x[b.index()].rearrange("(c p) d -> p c d", p=P) if b.reg is None else \
                x[bass.ds(b.index(), 1), :, :].rearrange("o (c p) d -> p (o c) d", p=P)

        def out_rows(b):
            return out[b.index()].rearrange("(c p) d -> p c d", p=P) if b.reg is None else \
                out[bass.ds(b.index(), 1), :, :].rearrange("o (c p) d -> p (o c) d", p=P)

        def mix_z(eng, b):
            for k in range(NK):
                if eng is PE:
                    wait(PE, "xT_lo", b)
                    ps = mix_bank(b, f"z{k}")
                    w = slice(k * P, (k + 1) * P)
                    sig("ps_z", mm3(ps[:, :], [(wz_hi[:, w], wz_lo[:, w], xT_hi[:, :], xT_lo[:, :])]))
                if eng is AC:
                    wait(AC, "ps_z", b, k + 1)
                    wait(AC, "ps_intra", b.prev())
                    sig("tanh", AC.activation(silu[:, k, :], bank_of(f"z{k}")[:, :], ACT.Tanh, scale=0.5))
                if eng is DVE:
                    wait(DVE, "tanh", b, k + 1)
                    sig("silu", DVE.scalar_tensor_tensor(silu[:, k, :], silu[:, k, :], 1.0, bank_of(f"z{k}")[:, :],
                                                         ALU.add, ALU.mult))

        def mix_silu_split(eng, b):
            for k in range(NK):
                if eng is AC:
                    wait(AC, "silu", b, k + 1)
                    wait(AC, "ps_y", b.prev().prev())
                    sig("silu_hi", AC.copy(sp_hi[:, k, :], silu[:, k, :]))
                if eng is PO:
                    wait(PO, "silu_hi", b, k + 1)
                    sig("silu_lo", PO.tensor_tensor(sp_lo[:, k, :], silu[:, k, :], sp_hi[:, k, :].bitcast(F32),
                                                    ALU.subtract))

        def mix_X(eng, b, cs):
            for c in cs:
                if eng is PE:
                    ps = mix_bank(b, f"X{c}")
                    sig("ps_X", mm3(ps[:, :], [(xT_hi[:, tok(c)], xT_lo[:, tok(c)], wx_hi[:, :], wx_lo[:, :])]))
                if eng is DVE:
                    wait(DVE, "ps_X", b, c + 1)
                    wait(DVE, "ps_intra", b.prev())
                    wait(DVE, "a_split", b)
                    sig("Xd", DVE.tensor_tensor(
                        Xd[:, c, :].rearrange("p (h n) -> p h n", h=H),
                        bank_of(f"X{c}")[:, :].rearrange("p (h n) -> p h n", h=H),
                        delta[:, c, :].unsqueeze(2).to_broadcast([P, H, HD]), ALU.mult))

        def mix_zg(eng, b):
            for q in range(NQ):
                if eng is PE:
                    wait(PE, "silu_lo", b)
                    ps = mix_bank(b, f"zg{q}")
                    w = slice(q * P, (q + 1) * P)
                    sig("ps_zg", mm3(ps[:, :], [(wzg_hi[:, k, w], wzg_lo[:, k, w], sp_hi[:, k, :], sp_lo[:, k, :])
                                                for k in range(NK)]))
                if eng is AC:
                    wait(AC, "ps_zg", b, q + 1)
                    wait(AC, "ps_out", b.prev())
                    sig("zg", AC.copy(zg[:, q, :], bank_of(f"zg{q}")[:, :]))

        def mix_scores(eng, b):
            if eng is PE:
                wait(PE, "a_split", b)
                ps = mix_bank(b, "cum")
                for c in range(1, NC):
                    last = PE.matmul(ps[DTROW:DTROW + H, tok(c - 1)], a[:, c, :], upper[:, :], start=True, stop=True)
                sig("ps_cum", last)
                ps = mix_bank(b, "ends")
                for part, first in ((a_hi, True), (a_lo, False)):
                    PE.matmul(ps[:, 0:(NC - 1) * H], strict_r[:, :], part[:, 0:NC - 1, :].rearrange("p c h -> p (c h)"),
                              start=first, stop=not first)
                sig("ps_ends", PE.matmul(ps[0:NS, 64:64 + NC * H], upper[:, P - 1:P].to_broadcast([P, NS]),
                                         a[:, :, :].rearrange("p c h -> p (c h)"),
                                         start=True, stop=True))
                wait(PE, "BC", b)
                ps = mix_bank(b, "G")
                for c in range(NC):
                    last = PE.matmul(ps[:, tok(c)], BT[:, tok(c)], CT[:, tok(c)], start=True, stop=True)
                sig("ps_G", last)
            R = slice(DTROW, DTROW + H)
            cols = (NC - 1) * P
            if eng is DVE:
                wait(DVE, "ps_G", b)
                wait(DVE, "W", b.prev())
                sig("Gm", DVE.tensor_tensor(Gm[:, :, :], bank_of("G")[:, :].rearrange("p (c t) -> p c t", c=NC),
                                            upper[:, :].unsqueeze(1).to_broadcast([P, NC, P]), ALU.mult))
                wait(DVE, "cumexp", b)
                wait(DVE, "ps_decb", b.prev())
                sig("cum_hi", DVE.tensor_copy(rows_s[R, 0:cols], rows[R, 0:cols]))
                wait(DVE, "cum_hi", b)
                sig("cum_lo", DVE.tensor_tensor(rows_s[DTROW + LOROW:DTROW + LOROW + H, 0:cols], rows[R, 0:cols],
                                                rows_s[R, 0:cols].bitcast(F32), ALU.subtract))
            if eng is AC:
                wait(AC, "ps_cum", b)
                wait(AC, "cum_lo", b.prev())
                sig("cumexp", AC.activation(rows[R, 0:cols], bank_of("cum")[R, 0:cols], ACT.Exp))
                wait(AC, "ps_ends", b)
                wait(AC, "Xde", b.prev())
                wait(AC, "state", b.prev())
                AC.activation(ends[:, :], bank_of("ends")[:, 0:(NC - 1) * H], ACT.Exp)
                sig("ends", AC.activation(total[:, :], bank_of("ends")[0:NS, 64:64 + NC * H], ACT.Exp))
            if eng is PO:
                for c in range(NC - 1):
                    wait(PO, "ends", b)
                    wait(PO, "Xd", b, c + 1)
                    wait(PO, "silu_lo", b)
                    sig("Xde", PO.tensor_tensor(
                        Xde[:, c, :].rearrange("p (h n) -> p h n", h=H), Xd[:, c, :].rearrange("p (h n) -> p h n", h=H),
                        ends[:, c * H:(c + 1) * H].unsqueeze(2).to_broadcast([P, H, HD]), ALU.mult))

        def mix_states(eng, b):
            low, high = slice(0, NS), slice(NS, 2 * NS)
            place = (("st01", low, 1), ("st01", high, 1), ("st2", low, 2))
            if eng is PE:
                for c, (use, half, _) in enumerate(place):
                    if c != 1:
                        wait(PE, "Xde", b, 2 if c == 0 else 3)
                        ps = mix_bank(b, use)
                    last = PE.matmul(ps[half, :], B_tok[:, c, :], Xde[:, c, :], start=True, stop=True)
                    if c > 0:
                        sig("ps_st", last)
            if eng is DVE:
                for c, (use, half, k) in enumerate(place):
                    ps = bank_of(use)[half, :]
                    wait(DVE, "ps_st", b, k)
                    wait(DVE, "ps_inter", b.prev())
                    if c == 0:
                        sig("state", DVE.tensor_copy(S[low, 0, :], ps))
                    else:
                        wait(DVE, "state", b, c)
                        sig("st_tmp", DVE.tensor_tensor(
                            S[half, c, :].rearrange("p (h n) -> p h n", h=H),
                            S[low, c - 1, :].rearrange("p (h n) -> p h n", h=H),
                            total[:, c * H:(c + 1) * H].unsqueeze(2).to_broadcast([NS, H, HD]), ALU.mult))
                        wait(DVE, "st_tmp", b, c)
                        sig("state", DVE.tensor_tensor(S[low, c, :], S[half, c, :], ps, ALU.add))

        def mix_mask(eng, b, u, both=PO):
            HF = NC // 2
            q, f = divmod(u, 2)
            shape = [P, HF, 2, P]
            for on, name, dst, src in ((PO, "Ua", Ua_hi, a_hi), (both, "Ua_lo", Ua_lo, a_lo)):
                if eng is on:
                    wait(on, "a_split", b)
                    wait(on, "ps_seg", b if u else b.prev(), u if u else None)
                    sig(name, on.tensor_tensor(dst[:, :].rearrange("p (c j t) -> p c j t", c=HF, j=2),
                                               upper[:, :].unsqueeze(1).unsqueeze(1).to_broadcast(shape),
                                               src[:, f * HF:(f + 1) * HF, 2 * q:2 * q + 2].bitcast(F32).unsqueeze(3)
                                               .to_broadcast(shape), ALU.mult))

        def mix_decay(eng, b, u, lo_on=PO):
            q, f = divmod(u, 2)
            HF = NC // 2
            cs = slice(f * HF, (f + 1) * HF)
            half = slice(f * T, (f + 1) * T)
            if eng is PE:
                wait(PE, "Ua", b, u + 1)
                wait(PE, "Ua_lo", b, u + 1)
                ps = mix_bank(b, f"seg{u}")
                PE.matmul(ps[:, :], strict_r[:, :], Ua_hi[:, :], start=True, stop=False)
                sig("ps_seg", PE.matmul(ps[:, :], strict_r[:, :], Ua_lo[:, :], start=False, stop=True))
            if u + 1 < 2 * NQ:
                mix_mask(eng, b, u + 1, lo_on)
            if eng is AC:
                wait(AC, "ps_seg", b, u + 1)
                wait(AC, "ps_st", b)
                if q >= 2:
                    wait(AC, "ps_intra", b, q - 1)
                sig("segexp", AC.activation(Wt[:, q % 2, half], bank_of(f"seg{u}")[:, :], ACT.Exp))
            if eng is DVE:
                wait(DVE, "segexp", b, u + 1)
                wv = Wt[:, q % 2, half].rearrange("p (c j t) -> p c j t", c=HF, j=2)
                sig("W", DVE.tensor_tensor(wv, wv, Gm[:, cs, :].unsqueeze(2).to_broadcast([P, HF, 2, P]), ALU.mult))

        def mix_from_start(eng, b, q):
            R = slice(DTROW, DTROW + LOROW + H)
            cols = (NC - 1) * P
            if eng is PE:
                wait(PE, "cum_lo", b)
                ps = mix_bank(b, f"decb{q}")
                sig("ps_decb", PE.matmul(ps[:, 0:cols], pairs[R, q * P:(q + 1) * P], rows_s[R, 0:cols], start=True, stop=True))
            if eng is AC:
                wait(AC, "ps_decb", b, q + 1)
                wait(AC, "skip", b if q else b.prev(), q if q else None)
                sig("decb", AC.copy(decb[:, P:T], bank_of(f"decb{q}")[:, 0:cols]))

        def mix_skip(eng, b, q):
            if eng is PE:
                wait(PE, "state", b)
                ps = mix_bank(b, f"inter{q}")
                for c in range(1, NC):
                    last = PE.matmul(ps[:, tok(c)], S[0:NS, c - 1, q * P:(q + 1) * P], CT[:, tok(c)], start=True, stop=True)
                sig("ps_inter", last)
                ps = mix_bank(b, f"XT{q}")
                w = slice(q * P, (q + 1) * P)
                sig("ps_XT", mm3(ps[:, :], [(wx_hi[:, w], wx_lo[:, w], xT_hi[:, :], xT_lo[:, :])]))
            if eng is DVE:
                wait(DVE, "ps_inter", b, q + 1)
                wait(DVE, "decb", b, q + 1)
                sig("inter", DVE.tensor_tensor(decb[:, P:T], bank_of(f"inter{q}")[:, P:T], decb[:, P:T], ALU.mult))
                wait(DVE, "ps_XT", b, q + 1)
                wait(DVE, "inter", b, q + 1)
                wait(DVE, "gated", b if q else b.prev(), q if q else None)
                sig("skip", DVE.scalar_tensor_tensor(yt[:, :], bank_of(f"XT{q}")[:, :], d_col[:, q:q + 1], decb[:, :],
                                                     ALU.mult, ALU.add))

        def mix_intra(eng, b, q):
            if eng is PE:
                wait(PE, "W", b, 2 * q + 2)
                ps = mix_bank(b, f"intra{q}")
                for c in range(NC):
                    for j in range(2):
                        h = 2 * q + j
                        at = (c * 2 + j) * P
                        last = PE.matmul(ps[j * HD:(j + 1) * HD, tok(c)], Xd[:, c, h * HD:(h + 1) * HD],
                                         Wt[:, q % 2, at:at + P], start=True, stop=True)
                sig("ps_intra", last)
            if eng is DVE:
                wait(DVE, "ps_intra", b, q + 1)
                wait(DVE, "skip", b, q + 1)
                sig("y", DVE.tensor_tensor(yt[:, :], bank_of(f"intra{q}")[:, :], yt[:, :], ALU.add))
                wait(DVE, "y", b, q + 1)
                wait(DVE, "zg", b, q + 1)
                sig("gated", DVE.tensor_tensor(zg[:, q, :], yt[:, :], zg[:, q, :], ALU.mult))

        def mix_out(eng, b):
            if eng is PE:
                wait(PE, "gated", b)
                ps = mix_bank(b, "out")
                for c in range(NC):
                    for q in range(NQ):
                        last = PE.matmul(ps[:, tok(c)], zg[:, q, tok(c)], wout[:, q, :], start=(q == 0), stop=(q == NQ - 1))
                sig("ps_out", last)
            if eng is DVE:
                wait(DVE, "ps_out", b)
                sig("v", DVE.tensor_tensor(x_in[:, :, :], bank_of("out")[:, :].rearrange("p (c d) -> p c d", c=NC),
                                           x_in[:, :, :], ALU.add))

        def norm_stats(eng, b, pre, src):
            veps, lnv, r0 = (nrm[:, k, :] for k in range(3))
            if eng is DVE:
                n = [0]
                for c in range(NC):
                    last = DVE.bn_stats(st6[:, c, :], src[:, c, :])
                link(DVE, pre + "_v", b, last, n)
                alone(DVE)
                for c in range(NC):
                    last = DVE.bn_aggr(mv[:, c, :], st6[:, c, :])
                link(DVE, pre + "_v", b, last, n)
                sig(pre + "_v", DVE.tensor_scalar(veps, mv[:, :, 1], LN_EPS, None, ALU.add))
            if eng is AC:
                wait(AC, pre + "_v", b, 3)
                sig(pre + "_s", AC.activation(lnv, veps, ACT.Ln))
                wait(AC, pre + "_s", b, 1)
                sig(pre + "_s", AC.activation(r0, lnv, ACT.Exp, scale=-0.5))

        def norm_apply(eng, b, pre, src, dst, done, before_write):
            veps, lnv, r0, t0, t1, rstd = (nrm[:, k, :] for k in range(6))
            if eng is DVE:
                n = [3]
                wait(DVE, pre + "_v", b, 3)
                wait(DVE, pre + "_s", b)
                link(DVE, pre + "_v", b, DVE.tensor_tensor(t0, r0, r0, ALU.mult), n)
                link(DVE, pre + "_v", b, DVE.tensor_tensor(t1, t0, veps, ALU.mult), n)
                link(DVE, pre + "_v", b, DVE.tensor_scalar(t0, t1, -0.5, 1.5, ALU.mult, ALU.add), n)
                link(DVE, pre + "_v", b, DVE.tensor_tensor(rstd, r0, t0, ALU.mult), n)
                before_write()
                for c in range(NC):
                    last = DVE.tensor_scalar(dst[:, c, :], src[:, c, :], mv[:, c, 0:1], rstd[:, c:c + 1],
                                             ALU.subtract, ALU.mult)
                sig(done, last)
                wait(DVE, done, b)

        def route_norm(eng, b):
            if eng is DVE:
                wait(DVE, "v", b)
            norm_stats(eng, b, "ln1", x_in)
            norm_apply(eng, b, "ln1", x_in, x1, "x1", lambda: wait(DVE, "acc", b.prev()))

        def route_transpose(eng, b):
            if eng is PE:
                wait(PE, "x1", b)
                wait(PE, "acc", b.prev())
                for c in range(NC):
                    last = PE.transpose(rb[:, tok(c)], x1[:, c, :], ident[:, :])
                sig("ps_x1T", last)
            if eng is AC:
                wait(AC, "ps_x1T", b)
                wait(AC, "xw", b.prev())
                sig("x1T", AC.copy(x1T, rb[:, :]))

        def route_logits(eng, b):
            if eng is PE:
                wait(PE, "x1T", b)
                for c in range(NC):
                    last = PE.matmul(rb[:, tok(c)], x1T[:, tok(c)], router[:, :], start=True, stop=True)
                sig("ps_lg", last)
            if eng is AC:
                wait(AC, "ps_lg", b)
                wait(AC, "gelu_hi", b.prev())
                wait(AC, "gelu_lo", b.prev())
                wait(AC, "gelu_lo_v", b.prev())
                sig("lg", AC.copy(lg[:, :, :].rearrange("p (c r) e -> p c (r e)", c=NC),
                                  rb[:, :].rearrange("p (c n) -> p c n", c=NC)[:, :, 0:NR * E]))

        def route_weights(eng, b):
            NGR = NC * NR
            wide3 = [P, NGR, E]
            if eng is DVE:
                n = [0]
                wait(DVE, "lg", b)
                wait(DVE, "gelu_lo", b.prev())
                alone(DVE)
                for g in range(NGR):
                    last = DVE.max(mx[:, g, :], lg[:, g, :])
                link(DVE, "rt_v", b, last, n)
                alone(DVE)
                for g in range(NGR):
                    last = DVE.max_index(ix[:, g, :], mx[:, g, :], lg[:, g, :])
                link(DVE, "rt_v", b, last, n)
                link(DVE, "rt_v", b, DVE.tensor_tensor(lg[:, :, :], lg[:, :, :], mx[:, :, 0:1].to_broadcast(wide3),
                                                       ALU.subtract), n)
                for k in range(TOPK):
                    last = DVE.tensor_tensor(hot[:, k, :, :], iota_e[:, :].unsqueeze(1).to_broadcast(wide3),
                                             ix[:, :, k:k + 1].to_broadcast(wide3), ALU.is_equal)
                link(DVE, "rt_v", b, last, n)
                link(DVE, "rt_v", b, DVE.tensor_tensor(hot[:, 0], hot[:, 0], hot[:, 1], ALU.add), n)
                link(DVE, "rt_v", b, DVE.tensor_tensor(hot[:, 0], hot[:, 0], hot[:, 2], ALU.add), n)
                wait(DVE, "rt_s", b)
                link(DVE, "rt_v", b, DVE.tensor_tensor(lg[:, :, :], lg[:, :, :], hot[:, 0], ALU.mult), n)
                link(DVE, "rt_v", b, DVE.tensor_reduce(ssum[:, :], lg[:, :, :], AX.X, ALU.add), n)
                wait(DVE, "ps_dwT", b.prev())
                sig("dw", DVE.reciprocal(srec[:, :], ssum[:, :]))
                wait(DVE, "dw", b)
                lv = lg[:, :, :].rearrange("p (c r) e -> p c r e", c=NC)
                rv = srec[:, :].rearrange("p (c r) -> p c r", c=NC)
                for r, dst in ((0, dwpad[:, :, 0:E]), (1, dw2_new[:, :, :]), (2, dwpad[:, :, B2ROW:B2ROW + E])):
                    last = DVE.tensor_tensor(dst, lv[:, :, r, :], rv[:, :, r:r + 1].to_broadcast([P, NC, E]), ALU.mult)
                sig("dwr", last)
            if eng is AC:
                wait(AC, "rt_v", b, 3)
                sig("rt_s", AC.activation(lg[:, :, :], lg[:, :, :], ACT.Exp))

        def route_rows(eng, b):
            R1 = slice(0, E)
            if eng is PE:
                wait(PE, "lg", b)
                wait(PE, "dwr", b)
                alone(PE)
                for c in range(NC):
                    last = PE.transpose(rb[0:DTROW, tok(c)], dwpad[:, c, :], ident[:, :])
                sig("ps_dwT", last)
            if eng is AC:
                wait(AC, "ps_dwT", b)
                wait(AC, "ps_b2", b.prev())
                sig("dwT", AC.copy(rows[0:DTROW, :], rb[0:DTROW, :]))
            if eng is DVE:
                wait(DVE, "dwT", b)
                wait(DVE, "ps_row", b.prev())
                sig("dw_hi", DVE.tensor_copy(rows_s[R1, :], rows[R1, :]))
                wait(DVE, "dw_hi", b)
                sig("dw_lo", DVE.tensor_tensor(rows_s[LOROW:LOROW + E, :], rows[R1, :], rows_s[R1, :].bitcast(F32), ALU.subtract))

        def expert_prep(eng, b, e):
            expert_row(eng, b, e)
            expert_split(eng, b, e)

        def expert_row(eng, b, e):
            if eng is PE:
                wait(PE, "dw_lo", b)
                if e == 0:
                    wait(PE, "dwT", b)
                else:
                    wait(PE, "xw", b, e)
                sel = pick[0:LOROW + E, e:e + 1].to_broadcast([LOROW + E, P])
                sig("ps_row", PE.matmul(rb[:, :], sel, rows_s[0:LOROW + E, :], start=True, stop=True))
            if eng is DVE:
                wait(DVE, "ps_row", b, e + 1)
                if e >= 2:
                    wait(DVE, "xw_hi", b, e - 1)
                    wait(DVE, "xw_lo", b, e - 1)
                sig("xw", DVE.tensor_tensor(wide[e % 2], rb[:, :], x1T, ALU.mult))

        def expert_split(eng, b, e):
            at = (e + 2) % NH
            if eng is AC:
                wait(AC, "xw", b, e + 1)
                wait(AC, "ps_y", b.prev())
                if e >= 4:
                    wait(AC, "ps_h", b, e - 3)
                elif e >= 2 and (b.reg is not None or b.off < NB - 1):
                    wait(AC, "ps_zg", Batch(b.reg, b.off + 1))
                sig("xw_hi", AC.copy(sp_hi[:, at, :], wide[e % 2]))
            if eng is PO:
                wait(PO, "xw_hi", b, e + 1)
                sig("xw_lo", PO.tensor_tensor(sp_lo[:, at, :], wide[e % 2], sp_hi[:, at, :].bitcast(F32), ALU.subtract))

        def expert_in(eng, b, e):
            if eng is PE:
                at = (e + 2) % NH
                if e == 0:
                    wait(PE, "comb", b.prev())
                wait(PE, "xw_lo", b, e + 1)
                for hc in range(NH):
                    w = slice(hc * P, (hc + 1) * P)
                    last = mm3(hb[hc][:, :], [(w1_hi[:, e, w], w1_lo[:, e, w], sp_hi[:, at, :], sp_lo[:, at, :])],
                               start=(e == 0), stop=(e == E - 1))
                    if e == E - 1:
                        sig("ps_h_full", last)
                if e < E - 1:
                    sig("ps_h", last)

        def expert_gelu(eng, b):
            for k in range(NH):
                g = wide[k % 2]
                if eng is AC:
                    wait(AC, "ps_h_full", b, k + 1)
                    if k >= 2:
                        wait(AC, "gelu_hi", b, k - 1)
                        wait(AC, ("gelu_lo", "gelu_lo_v")[k % 2], b, k // 2)
                    else:
                        wait(AC, "xw_hi", b)
                        wait(AC, "xw_lo", b)
                    sig("gelu", AC.activation(g, hb[k][:, :], ACT.Gelu))
                lo = (sp_lo[:, k, :], g, sp_hi[:, k, :].bitcast(F32), ALU.subtract)
                if eng is DVE:
                    wait(DVE, "ps_h_full", b)
                    wait(DVE, "gelu", b, k + 1)
                    sig("gelu_hi", DVE.tensor_copy(sp_hi[:, k, :], g))
                    if k % 2:
                        wait(DVE, "gelu_hi", b, k + 1)
                        sig("gelu_lo_v", DVE.tensor_tensor(*lo))
                if eng is PO and k % 2 == 0:
                    wait(PO, "gelu_hi", b, k + 1)
                    sig("gelu_lo", PO.tensor_tensor(*lo))

        def expert_b2(eng, b):
            R = slice(B2ROW, B2ROW + E)
            if eng is PE:
                wait(PE, "xw", b)
                for c in range(NC):
                    last = PE.matmul(rb[:, tok(c)], rows[R, tok(c)], b2_sb[R, :], start=True, stop=True)
                sig("ps_b2", last)
            if eng is DVE:
                wait(DVE, "ps_b2", b)
                wait(DVE, "stored", b.prev())
                DVE.tensor_copy(dw2[:, :, :], dw2_new[:, :, :])
                sig("acc", DVE.tensor_tensor(acc[:, :, :], rb[:, :].rearrange("p (c d) -> p c d", c=NC), x1, ALU.add))
                wait(DVE, "acc", b)

        def expert_out(eng, b, c, gs=range(NG)):
            per = E + 1
            for g in gs:
                m = c * NG + g
                if eng is PE:
                    if m < NH:
                        wait(PE, "gelu", b, m + 1)
                    else:
                        before = m - NH
                        wait(PE, "comb", b, before // NG * per + (before % NG + 1) * EG)
                    w = slice(g * T, (g + 1) * T)

                    def gelu_ready(k):
                        if m == 0:
                            wait(PE, ("gelu_lo", "gelu_lo_v")[k % 2], b, k // 2 + 1)
                    sig("ps_y", mm3(hb[m % NH][:, :], [(sp_hi[:, k, tok(c)], sp_lo[:, k, tok(c)], w2_hi[:, k, w], w2_lo[:, k, w])
                                                       for k in range(NH)], before=gelu_ready))
                if eng is DVE:
                    wait(DVE, "ps_y", b, m + 1)
                    for s in range(EG):
                        e = g * EG + s
                        n = c * per + e
                        ps, w, dst = hb[m % NH][:, s * D:(s + 1) * D], dw2[:, c, e:e + 1], (acc[:, c, :], acc_odd[:, :])[e % 2]
                        if e >= 2:
                            wait(DVE, "comb", b, n - 1)
                        if e == 1:
                            sig("comb", DVE.tensor_scalar(dst, ps, w, None, ALU.mult))
                        else:
                            sig("comb", DVE.scalar_tensor_tensor(dst, ps, w, dst, ALU.mult, ALU.add))
            if eng is DVE and NG - 1 in gs:
                wait(DVE, "comb", b, (c + 1) * per - 1)
                sig("comb", DVE.tensor_tensor(acc[:, c, :], acc[:, c, :], acc_odd[:, :], ALU.add))
                wait(DVE, "comb", b, (c + 1) * per)

        def expert_norm_stats(eng, b):
            if eng is DVE:
                wait(DVE, "comb", b)
            norm_stats(eng, b, "ln2", acc)

        def expert_norm(eng, b):
            norm_apply(eng, b, "ln2", acc, acc, "o", lambda: None)
            store(eng, b)

        def store(eng, b):
            if eng is SP:
                wait(SP, "o", b)
                sig("stored", SP.dma_start(out_rows(b), acc[:, :, :]))

        def experts(eng, b, es, ahead):
            for e in es:
                while ahead[0] <= min(e + 2, E - 1):
                    expert_prep(eng, b, ahead[0])
                    ahead[0] += 1
                expert_in(eng, b, e)

        def body(eng, b, front_next, norm_before=True):
            p, nxt = b.prev(), Batch(b.reg, b.off + 1)
            ahead = [4]
            expert_split(eng, p, 0)
            mix_silu_split(eng, b)
            mix_X(eng, b, range(1, NC))
            expert_prep(eng, p, 1)
            expert_in(eng, p, 0)
            mix_zg(eng, b)
            expert_prep(eng, p, 2)
            expert_in(eng, p, 1)
            expert_row(eng, p, 3)
            mix_scores(eng, b)
            expert_split(eng, p, 3)
            if norm_before:
                expert_norm_stats(eng, p.prev())
            experts(eng, p, [2], ahead)
            mix_states(eng, b)
            mix_decay(eng, b, 0)
            e = 3
            for q in range(NQ):
                if q == 0:
                    expert_row(eng, p, e + 2)
                    expert_in(eng, p, e)
                    mix_from_start(eng, b, q)
                else:
                    mix_from_start(eng, b, q)
                    experts(eng, p, [e], ahead)
                if q == 0 and norm_before:
                    expert_norm(eng, p.prev())
                mix_skip(eng, b, q)
                mix_decay(eng, b, 2 * q + 1)
                if q == 0:
                    expert_split(eng, p, e + 2)
                    ahead[0] += 1
                experts(eng, p, [e + 1], ahead)
                e += 2
                if q < NQ - 1:
                    mix_decay(eng, b, 2 * q + 2)
                mix_intra(eng, b, q)
            experts(eng, p, range(e, E), ahead)
            expert_gelu(eng, p)
            expert_b2(eng, p)
            mix_out(eng, b)
            route_norm(eng, b)
            expert_out(eng, p, 0)
            if front_next:
                mix_load_next(eng, b)
            route_transpose(eng, b)
            expert_out(eng, p, 1)
            route_logits(eng, b)
            if front_next:
                mix_x(eng, nxt)
            route_weights(eng, b)
            expert_out(eng, p, 2)
            if front_next:
                mix_dt(eng, nxt)
                mix_bc(eng, nxt)
            route_rows(eng, b)
            if front_next:
                mix_mask(eng, nxt, 0)
                mix_z(eng, nxt)
            expert_out(eng, p, 3, range(0, NG - 1))
            expert_row(eng, b, 0)
            if front_next:
                mix_X(eng, nxt, [0])
            expert_out(eng, p, 3, range(NG - 1, NG))

        def mixer_alone(eng, b):
            mix_x(eng, b)
            neg_a_ready(eng)
            if eng is PE:
                PE.wait_ge(sems["wbdt"], 2)
            mix_dt(eng, b)
            if eng is PE:
                PE.wait_ge(sems["cast"], 8 + NC)
            mix_bc(eng, b)
            mix_z(eng, b)
            mix_silu_split(eng, b)
            mix_X(eng, b, range(NC))
            router_product(eng)
            mix_zg(eng, b)
            mix_mask(eng, b, 0, DVE)
            mix_scores(eng, b)
            split_expert_weights(eng, range(0, 4))
            mix_states(eng, b)
            mix_decay(eng, b, 0, DVE)
            k = 4
            for q in range(NQ):
                mix_from_start(eng, b, q)
                mix_skip(eng, b, q)
                mix_decay(eng, b, 2 * q + 1, DVE)
                split_expert_weights(eng, range(k, k + 2))
                if q < NQ - 1:
                    mix_decay(eng, b, 2 * q + 2, DVE)
                mix_intra(eng, b, q)
                split_expert_weights(eng, range(k + 2, k + 4))
                k += 4
            split_expert_weights(eng, range(k, NW))
            mix_out(eng, b)
            expert_weights_ready(eng)
            route_norm(eng, b)
            mix_load_next(eng, b)
            route_transpose(eng, b)
            route_logits(eng, b)
            nxt = Batch(None, 1)
            mix_x(eng, nxt)
            route_weights(eng, b)
            mix_dt(eng, nxt)
            mix_bc(eng, nxt)
            route_rows(eng, b)
            mix_mask(eng, nxt, 0)
            mix_z(eng, nxt)
            expert_row(eng, b, 0)
            mix_X(eng, nxt, [0])

        def mixture_alone(eng, b):
            ahead = [4]
            expert_split(eng, b, 0)
            expert_prep(eng, b, 1)
            expert_in(eng, b, 0)
            expert_prep(eng, b, 2)
            expert_in(eng, b, 1)
            expert_prep(eng, b, 3)
            experts(eng, b, [2, 3], ahead)
            expert_norm_stats(eng, b.prev())
            experts(eng, b, [4, 5], ahead)
            expert_norm(eng, b.prev())
            experts(eng, b, range(6, E), ahead)
            expert_gelu(eng, b)
            expert_b2(eng, b)
            for c in range(NC):
                expert_out(eng, b, c)
            expert_norm_stats(eng, b)
            expert_norm(eng, b)

        def program(eng):
            waited[id(eng)] = {}
            setup(eng)
            mixer_alone(eng, Batch(None, 0))
            body(eng, Batch(None, 1), True, norm_before=False)
            waited[id(eng)] = {}
            with eng.Fori(2, NB - 1) as i:
                body(eng, Batch(i, 0), True)
            waited[id(eng)] = {}
            body(eng, Batch(None, NB - 1), False)
            mixture_alone(eng, Batch(None, NB - 1))
            if eng is SP:
                wait(SP, "stored", Batch(None, NB - 1))

        product("dwr", 1)
        block = ctx.enter_context(nc.Block())

        @block.sync
        def _(eng):
            program(SP)

        @block.tensor
        def _(eng):
            program(PE)

        @block.vector
        def _(eng):
            program(DVE)

        @block.scalar
        def _(eng):
            program(AC)

        @block.gpsimd
        def _(eng):
            program(PO)

        for p in prods.values():
            written = 3 if p.name != "x_in" else 2
            assert p.done % p.n == 0 and p.done // p.n >= written, (p.name, p.done, p.n)


def kernel(L0_attn_x, L0_attn_Wz, L0_attn_Win, L0_attn_Wzg, L0_attn_Wout, L0_attn_dt_bias, L0_attn_A_log,
           L0_attn_D_param, L0_ffn_P_w, L0_ffn_U1, L0_ffn_U2, L0_ffn_U3, L0_ffn_W1, L0_ffn_W2, L0_ffn_b2):
    import concourse.bacc as bacc
    from concourse.bass_utils import run_bass_kernel_spmd

    lay = np.ascontiguousarray
    w2 = np.asarray(L0_ffn_W2)
    arrays = dict(
        x=lay(L0_attn_x), Wz=lay(L0_attn_Wz), Win=lay(L0_attn_Win), Wzg=lay(L0_attn_Wzg), Wout=lay(L0_attn_Wout),
        dt_bias=lay(L0_attn_dt_bias), A_log=lay(L0_attn_A_log), D_param=lay(L0_attn_D_param), P_w=lay(L0_ffn_P_w),
        U1T=lay(np.asarray(L0_ffn_U1).T), U2T=lay(np.asarray(L0_ffn_U2).T), U3T=lay(np.asarray(L0_ffn_U3).T),
        W1T=lay(np.asarray(L0_ffn_W1).transpose(2, 0, 1)),
        W2T=lay(w2.transpose(2, 0, 1).reshape(w2.shape[2], -1)),
        b2=lay(L0_ffn_b2),
    )
    nc = bacc.Bacc("TRN2", target_bir_lowering=False, num_devices=1)
    aps = [nc.dram_tensor("in_" + k, v.shape, mybir.dt.from_np(v.dtype), kind="ExternalInput").ap() for k, v in arrays.items()]
    res = nc.dram_tensor("result", (NB, T, D), F32, kind="ExternalOutput").ap()
    layer_program(nc, *aps, res)
    r = run_bass_kernel_spmd(nc, [{"in_" + k: v for k, v in arrays.items()}], core_ids=[0])
    return r.results[0]["result"]
```
